# Optimizing a Trainium2 kernel written in Bass

```python
import numpy as np
import jax
import jax.numpy as jnp

def _softmax(x, axis=-1):
    return jax.nn.softmax(x, axis=axis)

def _gelu(x):
    return jax.nn.gelu(x, approximate=True)

def _silu(x):
    return jax.nn.silu(x)

def _sigmoid(x):
    return jax.nn.sigmoid(x)

def _layernorm(x, axis=-1, eps=1e-05):
    m = jnp.mean(x, axis=axis, keepdims=True)
    v = jnp.var(x, axis=axis, keepdims=True)
    return (x - m) / jnp.sqrt(v + eps)

def _scatter_add(tgt, idx, src, axis=0):
    return tgt.at[idx].add(src)

def _segment_sum(src, seg, n):
    return jax.ops.segment_sum(src, seg, n)
kernel_name = 'mk_prb_d1_jaxref_r4_40ec00'

def setup_inputs(seed: int=0):
    np.random.seed(seed)
    _w = jnp.asarray

    def _L0_attn_setup():
        import jax, jax.numpy as jnp
        import numpy as np
        import math
        DIM = 512
        N_HEADS = 16
        N_KV_HEADS = 8
        HEAD_DIM = DIM // N_HEADS
        N_REP = N_HEADS // N_KV_HEADS
        BLOCK = 128
        TOPK = 8
        NEG_INF = -10000.0
        SEQ = 1024
        BS = 1

        def _rope_tables(seq_len, head_dim, base=10000.0):
            inv_freq = 1.0 / base ** (jnp.arange(0, head_dim, 2, dtype=jnp.float32) / head_dim)
            ang = jnp.arange(seq_len, dtype=jnp.float32)[:, None] * inv_freq[None, :]
            return (jnp.cos(ang), jnp.sin(ang))

        def _apply_rope(t, cos, sin):
            t1 = t[..., 0::2]
            t2 = t[..., 1::2]
            c = cos[None, :, None, :]
            s = sin[None, :, None, :]
            out_even = t1 * c - t2 * s
            out_odd = t1 * s + t2 * c
            out = jnp.stack([out_even, out_odd], axis=-1)
            return out.reshape(t.shape)
        key = jax.random.key(seed)
        ks = jax.random.split(key, 5)
        scale = 1.0 / math.sqrt(DIM)
        x = jax.random.normal(ks[0], (BS, SEQ, DIM), dtype=jnp.float32)
        wq = jax.random.normal(ks[1], (DIM, N_HEADS * HEAD_DIM), dtype=jnp.float32) * scale
        wk = jax.random.normal(ks[2], (DIM, N_KV_HEADS * HEAD_DIM), dtype=jnp.float32) * scale
        wv = jax.random.normal(ks[3], (DIM, N_KV_HEADS * HEAD_DIM), dtype=jnp.float32) * scale
        wo = jax.random.normal(ks[4], (DIM, DIM), dtype=jnp.float32) * scale
        return {'x': x, 'wq': wq, 'wk': wk, 'wv': wv, 'wo': wo}
    _L0_attn_in = _L0_attn_setup()

    def _L0_ffn_setup():
        import jax, jax.numpy as jnp
        import numpy as np
        D_MODEL = 512
        D_EXPERT = 2048
        EPS = 1e-08

        def ternary_quant(w):
            scale = jnp.mean(jnp.abs(w)) + EPS
            q = jnp.clip(jnp.round(w / scale), -1.0, 1.0) * scale
            return w + jax.lax.stop_gradient(q - w)
        key = jax.random.key(seed)
        k_x, k_up, k_gate, k_down = jax.random.split(key, 4)
        std_in = 1.0 / np.sqrt(D_MODEL)
        std_exp = 1.0 / np.sqrt(D_EXPERT)
        return {'x': jax.random.normal(k_x, (4, 512, D_MODEL), dtype=jnp.float32), 'W_up': jax.random.normal(k_up, (D_EXPERT, D_MODEL), dtype=jnp.float32) * std_in, 'W_gate': jax.random.normal(k_gate, (D_EXPERT, D_MODEL), dtype=jnp.float32) * std_in, 'W_down': jax.random.normal(k_down, (D_MODEL, D_EXPERT), dtype=jnp.float32) * std_exp}
    _L0_ffn_in = _L0_ffn_setup()
    _d = {'L0_attn_x': _L0_attn_in['x'], 'L0_attn_wq': _L0_attn_in['wq'], 'L0_attn_wk': _L0_attn_in['wk'], 'L0_attn_wv': _L0_attn_in['wv'], 'L0_attn_wo': _L0_attn_in['wo'], 'L0_ffn_W_up': _L0_ffn_in['W_up'], 'L0_ffn_W_gate': _L0_ffn_in['W_gate'], 'L0_ffn_W_down': _L0_ffn_in['W_down']}
    _x0 = _d['L0_attn_x']
    _d['L0_attn_x'] = jax.random.normal(jax.random.fold_in(jax.random.key(seed), 1), (4, 512, 512), dtype=_x0.dtype)
    del _x0
    return _d

def reference(L0_attn_x, L0_attn_wq, L0_attn_wk, L0_attn_wv, L0_attn_wo, L0_ffn_W_up, L0_ffn_W_gate, L0_ffn_W_down):

    def _L0_attn_ref(x, wq, wk, wv, wo):
        import jax, jax.numpy as jnp
        import numpy as np
        import math
        DIM = 512
        N_HEADS = 16
        N_KV_HEADS = 8
        HEAD_DIM = DIM // N_HEADS
        N_REP = N_HEADS // N_KV_HEADS
        BLOCK = 128
        TOPK = 8
        NEG_INF = -10000.0
        SEQ = 1024
        BS = 1

        def _rope_tables(seq_len, head_dim, base=10000.0):
            inv_freq = 1.0 / base ** (jnp.arange(0, head_dim, 2, dtype=jnp.float32) / head_dim)
            ang = jnp.arange(seq_len, dtype=jnp.float32)[:, None] * inv_freq[None, :]
            return (jnp.cos(ang), jnp.sin(ang))

        def _apply_rope(t, cos, sin):
            t1 = t[..., 0::2]
            t2 = t[..., 1::2]
            c = cos[None, :, None, :]
            s = sin[None, :, None, :]
            out_even = t1 * c - t2 * s
            out_odd = t1 * s + t2 * c
            out = jnp.stack([out_even, out_odd], axis=-1)
            return out.reshape(t.shape)
        bs, S, _ = x.shape
        inv_sqrt_d = 1.0 / math.sqrt(HEAD_DIM)
        q = (x @ wq).reshape(bs, S, N_HEADS, HEAD_DIM)
        k = (x @ wk).reshape(bs, S, N_KV_HEADS, HEAD_DIM)
        v = (x @ wv).reshape(bs, S, N_KV_HEADS, HEAD_DIM)
        cos, sin = _rope_tables(S, HEAD_DIM)
        q = _apply_rope(q, cos, sin)
        k = _apply_rope(k, cos, sin)
        q = jnp.transpose(q, (0, 2, 1, 3))
        k = jnp.transpose(k, (0, 2, 1, 3))
        v = jnp.transpose(v, (0, 2, 1, 3))
        k_e = jnp.repeat(k, N_REP, axis=1)
        v_e = jnp.repeat(v, N_REP, axis=1)
        num_blocks = S // BLOCK
        k_blocks = k_e.reshape(bs, N_HEADS, num_blocks, BLOCK, HEAD_DIM)
        block_means = k_blocks.mean(axis=3)
        gating = jnp.einsum('bhsd,bhnd->bhsn', q, block_means) * inv_sqrt_d
        q_block_idx = jnp.arange(S) // BLOCK
        future_block = q_block_idx[:, None] < jnp.arange(num_blocks)[None, :]
        gating = jnp.where(future_block[None, None], NEG_INF, gating)
        curr_k = min(TOPK, num_blocks)
        _, sel_idx = jax.lax.top_k(gating, curr_k)
        selected = jnp.sum(jax.nn.one_hot(sel_idx, num_blocks, dtype=jnp.float32), axis=-2) > 0
        token_keep = jnp.repeat(selected, BLOCK, axis=-1)[..., :S]
        token_mask = jnp.where(token_keep, 0.0, NEG_INF)
        scores = jnp.einsum('bhsd,bhtd->bhst', q, k_e) * inv_sqrt_d
        causal = jnp.triu(jnp.ones((S, S), dtype=jnp.float32), k=1)
        final_mask = jnp.maximum(token_mask, causal[None, None] * NEG_INF)
        scores = scores + final_mask
        probs = jax.nn.softmax(scores.astype(jnp.float32), axis=-1).astype(scores.dtype)
        out = jnp.einsum('bhst,bhtd->bhsd', probs, v_e)
        out = jnp.transpose(out, (0, 2, 1, 3)).reshape(bs, S, N_HEADS * HEAD_DIM)
        return out @ wo

    def _L0_ffn_ref(x, W_up, W_gate, W_down):
        import jax, jax.numpy as jnp
        import numpy as np
        D_MODEL = 512
        D_EXPERT = 2048
        EPS = 1e-08

        def ternary_quant(w):
            scale = jnp.mean(jnp.abs(w)) + EPS
            q = jnp.clip(jnp.round(w / scale), -1.0, 1.0) * scale
            return w + jax.lax.stop_gradient(q - w)
        wu = ternary_quant(W_up)
        wg = ternary_quant(W_gate)
        wd = ternary_quant(W_down)
        up = jnp.einsum('bsd,ed->bse', x, wu)
        gate = jnp.einsum('bsd,ed->bse', x, wg)
        hidden = jax.nn.silu(up) * gate
        return jnp.einsum('bse,de->bsd', hidden, wd)
    x = L0_attn_x
    xn = _layernorm(x, axis=-1)
    x = x + _L0_attn_ref(xn, L0_attn_wq, L0_attn_wk, L0_attn_wv, L0_attn_wo) + _L0_ffn_ref(xn, L0_ffn_W_up, L0_ffn_W_gate, L0_ffn_W_down)
    return x

_drawn_inputs = setup_inputs


def setup_inputs(seed=0):
    import zlib

    import numpy as np

    out = dict(_drawn_inputs(seed))
    spreads = {}
    factors = {}
    for name, (base, spread) in spreads.items():
        noise = np.random.default_rng([zlib.crc32(name.encode()), seed]).standard_normal(out[name].shape)
        drawn = base * np.exp(spread * noise) if base else spread * noise
        out[name] = jnp.asarray(drawn.astype(out[name].dtype))
    for name, factor in factors.items():
        out[name] = (out[name] * factor).astype(out[name].dtype)
    return out
```

```python
import concourse.bass as bass
from concourse import mybir
from contextlib import ExitStack
import numpy as np

F32 = mybir.dt.float32
F16 = mybir.dt.float16
U32 = mybir.dt.uint32
ALU = mybir.AluOpType
ACT = mybir.ActivationFunctionType
AX = mybir.AxisListType
RMAX = bass.bass_isa.ReduceOp.max
RADD = bass.bass_isa.ReduceOp.add

P = 128
B, S, D = 4, 512, 512
H, KV, HD = 16, 8, 32
HA = H + KV
E = 2048
C = D // P
T = S // P
ET = E // P
STK = 3 * HD
ROWS = STK + 2
EPS = 1e-5

X_UP = 11
W_UP = 14
MAX_DOWN = 9
H_DOWN = 4
MAX_GROUPS = H * T // 2


def build(nc, x, wq, wk, wv, wo, w_up_t, w_gate_t, w_down_t, rope_c, rope_s, ident_in, out):
    ctx = ExitStack()
    with ctx:
        def sb(name, shape, dt):
            return ctx.enter_context(nc.sbuf_tensor(name, shape, dt))

        def sem(name):
            return ctx.enter_context(nc.semaphore(name))

        def as16(ap):
            return ap.bitcast(F16)

        x_v = x.rearrange("b (t p) d -> b p t d", p=P)
        out_v = out.rearrange("b (t p) d -> b p t d", p=P)

        t_up = sb("t_up", [P, C, E], F16)
        t_gate = sb("t_gate", [P, C, E], F16)
        w_qkv = sb("w_qkv", [P, 2, C, 1024], F16)
        w_o = sb("w_o", [P, 2, C, D], F16)
        ident = sb("identity", [P, P], F16)
        cos_t = sb("cos_t", [P, T, HD], F32)
        sin_t = sb("sin_t", [P, T, HD], F32)
        v_all = sb("v_all", [P, T, KV, 2 * HD + 1], F16)
        xn_t = sb("xn_t", [P, 2, C, S], F16)
        x_in = sb("x_in", [P, T, D], F32)

        late = sb("late", [P, 8192], F32)
        t_down = as16(late[:, 0:4096]).rearrange("p (e d) -> p e d", e=ET)
        a_tok = as16(late[:, 4096:6144]).rearrange("p (s t d) -> p s t d", s=2, t=T)
        y = late[:, 6144:8192].rearrange("p (t d) -> p t d", t=T)

        hid_raw = sb("hid_raw", [P, 8192], F32)
        hid = as16(hid_raw[:, :]).rearrange("p (s e n) -> p s e n", s=2, e=ET)

        stk_raw = sb("stk_raw", [P, 6144], F32)
        stk = as16(stk_raw[:, :]).rearrange("p (h n) -> p h n", h=HA)
        w_raw = stk_raw[:, 0:4096].rearrange("p (c n) -> p c n", c=C)

        p32 = sb("p32", [P, 2, 2 * S], F32)
        ph = sb("ph", [P, 2, T, S], F16)
        pl = sb("pl", [P, 2, T, S], F16)
        rope_a = p32[:, 0, 0:HA * HD].rearrange("p (h d) -> p h d", d=HD)
        rope_b = p32[:, 1, 0:HA * HD].rearrange("p (h d) -> p h d", d=HD)
        xs32 = ph[:, 0, :, :].rearrange("p a b -> p (a b)").bitcast(F32).rearrange(
            "p (n d) -> p n d", n=2)
        x_tok = ph[:, 1, :, :].rearrange("p a (s d) -> p (a s) d", s=1).rearrange(
            "p (n s) d -> p n s d", n=2)
        pl_flat = pl[:, :, :, :].rearrange("p a b c -> p (a b c)")
        r32 = pl_flat[:, 0:2 * HA * HD].bitcast(F32).rearrange("p (h d) -> p h d", d=HD)
        tk = (pl_flat[:, 2 * HA * HD:2 * HA * HD + HA * STK].rearrange("p (h d) -> p h d", d=STK),
              ph[:, :, :, :].rearrange("p a b c -> p (a b c)")[:, 0:HA * STK].rearrange(
                  "p (h d) -> p h d", d=STK))

        act_raw = sb("act_raw", [P, 5, D], F32)
        th = act_raw[:, 0:2, :]
        t1 = act_raw[:, 2, :]
        h32 = act_raw[:, 3:5, :]
        a_t = act_raw[:, 0:4, :].rearrange("p a b -> p (a b)").bitcast(F16).rearrange(
            "p (s c n) -> p s c n", s=2, c=C)
        wo_raw = act_raw[:, 0:4, :]

        norm_e = sb("norm_e", [P, 2, T, HD], F32)
        norm_f = sb("norm_f", [P, 2, T, HD], F32)
        norm_a = sb("norm_a", [P, T, HD], F32)
        rden = sb("rden", [P, T, 1], F32)
        mx = sb("mx", [P, T, H], F32)
        m_tok = sb("m_tok", [P, T, 2, H], F16)
        m_row = sb("m_row", [2 * H, S], F16)
        stats = sb("stats", [P, T, 6], F32)
        mv = sb("mv", [P, T, 2], F32)
        rstd = sb("rstd", [P, 6, T], F32)
        sums = sb("sums", [P, 3, 2 * C], F32)
        part = sb("part", [P, 3], F32)
        total = sb("total", [P, 3], F32)
        scale = sb("scale", [P, 3], F32)
        theta = sb("theta", [P, 3], F32)
        ntheta = sb("ntheta", [P, 3], F32)
        wmax = sb("wmax", [P, 4], F32)
        wmax_all = sb("wmax_all", [P, 4], F32)
        wpow = sb("wpow", [P, 4], F32)
        winv = sb("winv", [P, 4], F32)
        coef = sb("coef", [P, 8], F32)
        one = sb("one", [P, 1], F32)
        spare = sb("spare", [P, 1], F32)
        minus_half = sb("minus_half", [P, T], F32)
        SC, TANH, CD, CA = (coef[:, n:n + 1] for n in (0, 1, 2, 3))
        WQ, WK, WV, WO = range(4)

        psum = ctx.enter_context(nc.psum_tensor("psum", [P, 8, 512], F32))
        BU, BG = 4, 5
        DOWN_BANK, WO_BANK = (4, 7, 6, 7), (6, 7, 6, 7)

        def bank16(n):
            return psum[:, n, :].bitcast(F16)

        names = """const_in wq_in wk_in wv_in wo_in x_in_s y_in y_out
            absmax_done absmax_all winv_done whi_done wlo_done
            sum_part sum_done sum_all theta_done neg_done up_t gate_t down_t coef_done setup
            mv_done eps_done pow_done newton rstd_done xs_ready xh_ready xl_ready xT_ready xnT_ready
            qkv_ready rope_step qkv_used r32_ready vh_done rhi_done rlo_done qkT_ready stack_done
            mx_ready mx_done mh_done ml_done mT_ready m_row_s m_rows
            sc_ready p32_ready exp_done pl_ready pv_done
            up_ready gate_ready tanh_done t1_done h32_ready hid_done
            rden_done e_done ef_done attn_done
            aT_ready attnT_ready down_ready wo_ready y1_done y_ready""".split()
        s = {n: sem(n) for n in names}
        (const_in, wq_in, wk_in, wv_in, wo_in, x_in_s, y_in, y_out,
         absmax_done, absmax_all, winv_done, whi_done, wlo_done,
         sum_part, sum_done, sum_all, theta_done, neg_done, up_t, gate_t, down_t, coef_done, setup,
         mv_done, eps_done, pow_done, newton, rstd_done, xs_ready, xh_ready, xl_ready, xT_ready,
         xnT_ready,
         qkv_ready, rope_step, qkv_used, r32_ready, vh_done, rhi_done, rlo_done, qkT_ready, stack_done,
         mx_ready, mx_done, mh_done, ml_done, mT_ready, m_row_s, m_rows,
         sc_ready, p32_ready, exp_done, pl_ready, pv_done,
         up_ready, gate_ready, tanh_done, t1_done, h32_ready, hid_done,
         rden_done, e_done, ef_done, attn_done,
         aT_ready, attnT_ready, down_ready, wo_ready, y1_done, y_ready) = (s[n] for n in names)

        up_in, gate_in, down_in = ([sem(f"{w}_in{c}") for c in range(C)] for w in ("up", "gate", "down"))
        winv_step, coef_step = sem("winv_step"), sem("coef_step")

        raws = (hid_raw, late, hid_raw)
        flat = (t_up[:, :, :].rearrange("p c e -> p (c e)"), t_gate[:, :, :].rearrange("p c e -> p (c e)"),
                as16(late[:, 0:4096]))
        arrived, turned = (up_in, gate_in, down_in), (up_t, gate_t, down_t)

        block = ctx.enter_context(nc.Block())

        def all_pairs(eng, b, pair):
            pair(b, 0)
            with eng.Fori(1, H // 2) as i:
                pair(b, i)

        def ge(eng, s, value):
            if not isinstance(value, int) or value > 0:
                eng.wait_ge(s, value)

        @block.sync
        def _(sp):
            sp.dma_start(x_in[:], x_v[0]).then_inc(x_in_s, 16)
            for w, s_in, lo, n in ((wq, wq_in, 0, 512), (wk, wk_in, 512, 256), (wv, wv_in, 768, 256)):
                sp.dma_start(w_raw[:, :, lo:lo + n], w.rearrange("(c p) n -> p c n", p=P)).then_inc(s_in, 16)
            sp.dma_start(ident[:], ident_in).then_inc(const_in, 16)
            sp.dma_start(cos_t[:], rope_c.rearrange("(t p) d -> p t d", p=P)).then_inc(const_in, 16)
            sp.dma_start(sin_t[:], rope_s.rearrange("(t p) d -> p t d", p=P)).then_inc(const_in, 16)
            for c in range(C):
                sp.dma_start(hid_raw[:, c * E:(c + 1) * E], w_up_t[c * P:(c + 1) * P, :]).then_inc(up_in[c], 16)
            for c in range(C):
                sp.dma_start(late[:, c * E:(c + 1) * E], w_gate_t[c * P:(c + 1) * P, :]).then_inc(gate_in[c], 16)
            sp.dma_start(wo_raw, wo.rearrange("(c p) n -> p c n", p=P)).then_inc(wo_in, 16)
            sp.wait_ge(xs_ready, T)
            sp.dma_start(x_in[:], x_v[1]).then_inc(x_in_s, 16)
            sp.wait_ge(up_t, C)
            down_v = w_down_t.rearrange("(e p) d -> p e d", p=P)
            hid_v = hid_raw[:, :].rearrange("p (e d) -> p e d", e=ET)
            for c in range(C):
                sp.dma_start(hid_v[:, c * 4:c * 4 + 4, :], down_v[:, c * 4:c * 4 + 4, :]).then_inc(down_in[c], 16)

            def rows_of_maxima(b):
                sp.wait_ge(m_row_s, b + 1)
                for part_ in range(2):
                    sp.dma_start(stk[STK + part_:STK + part_ + 1, 0:H, :],
                                 m_row[part_ * H:(part_ + 1) * H, :]).then_inc(m_rows, 16)

            rows_of_maxima(0)
            with sp.Fori(1, B) as b:
                ge(sp, y_out, (b - 1) * T * 16)
                sp.wait_ge(gate_t, C)
                sp.dma_start(y, x_v[b - 1]).then_inc(y_in, 16)
                sp.wait_ge(xs_ready, (b + 1) * T)
                sp.dma_start(x_in[:], x_v[(b + 1) % B]).then_inc(x_in_s, 16)
                rows_of_maxima(b)
                for t in range(T):
                    sp.wait_ge(y_ready, (b - 1) * T + t + 1)
                    sp.dma_start(out_v[b - 1, :, t, :], y[:, t, :]).then_inc(y_out, 16)
            sp.wait_ge(y_out, (B - 1) * T * 16)
            sp.dma_start(y, x_v[B - 1]).then_inc(y_in, 16)
            for t in range(T):
                sp.wait_ge(y_ready, (B - 1) * T + t + 1)
                sp.dma_start(out_v[B - 1, :, t, :], y[:, t, :]).then_inc(y_out, 16)
            sp.wait_ge(y_out, B * T * 16)

        def layernorm_rstd(pool, b=0):
            pool.wait_ge(eps_done, b + 1)
            nc.gpsimd.tensor_tensor(rstd[:, 1, :], rstd[:, 0, :], minus_half[:], ALU.pow).then_inc(pow_done, 1)

        def layernorm_lo(pool, b):
            for t in range(T):
                pool.wait_ge(xh_ready, b * T + t + 1)
                nc.gpsimd.tensor_tensor(x_tok[:, t % 2, 1, :], xs32[:, t % 2, :], x_tok[:, t % 2, 0, :],
                                        ALU.subtract).then_inc(xl_ready, 1)

        def rope_lo(pool, b, between=lambda t: None):
            for t in range(T):
                pool.wait_ge(rhi_done, b * T + t + 1)
                stack = tk[t % 2]
                nc.gpsimd.tensor_tensor(stack[:, 0:H, 2 * HD:3 * HD], r32[:, 0:H, :],
                                        stack[:, 0:H, HD:2 * HD], ALU.subtract)
                nc.gpsimd.tensor_tensor(stack[:, H:HA, 0:HD], r32[:, H:HA, :],
                                        stack[:, H:HA, HD:2 * HD], ALU.subtract).then_inc(rlo_done, 1)
                between(t)

        def hidden_pool(pool, n, j, e):
            pool.wait_ge(h32_ready, n + 1)
            nc.gpsimd.tensor_tensor(hid[:, 0, e, :], h32[:, j, :], one[:].to_broadcast([P, D]),
                                    ALU.mult).then_inc(hid_done, 1)
            pool.wait_ge(hid_done, 2 * n + 1)
            nc.gpsimd.tensor_tensor(hid[:, 1, e, :], h32[:, j, :], hid[:, 0, e, :],
                                    ALU.subtract).then_inc(hid_done, 1)

        def attn_pool(pool, n, j, h):
            pool.wait_ge(ef_done, n + 1)
            nc.gpsimd.tensor_tensor(norm_a[:], norm_e[:, j], norm_f[:, j], ALU.add)
            hi = a_tok[:, 0, :, bass.ts(h, HD)]
            lo = a_tok[:, 1, :, bass.ts(h, HD)]
            nc.gpsimd.tensor_tensor(hi, norm_e[:, j], norm_f[:, j], ALU.add).then_inc(attn_done, 1)
            pool.wait_ge(attn_done, 2 * n + 1)
            nc.gpsimd.tensor_tensor(lo, norm_a[:], hi, ALU.subtract).then_inc(attn_done, 1)

        def pair_pool(b, i):
            pool = nc.gpsimd
            n = (b * (H // 2) + i) * 2
            if isinstance(i, int) and i == 0:
                ge(pool, aT_ready, b * T)
            else:
                attn_pool(pool, n - 1, 1, i * 2 - 1)
            hidden_pool(pool, n, 0, i * 2)
            if isinstance(i, int):
                layernorm_rstd(pool, b + 1)
            attn_pool(pool, n, 0, i * 2)
            hidden_pool(pool, n + 1, 1, i * 2 + 1)

        def last_head_pool(pool, b):
            attn_pool(pool, b * H + H - 1, 1, H - 1)

        @block.gpsimd
        def _(pool):
            nc.gpsimd.memset(one[:], 1.0).then_inc(setup, 1)
            nc.gpsimd.memset(minus_half[:], -0.5).then_inc(setup, 1)
            nc.gpsimd.memset(v_all[:, :, :, 2 * HD:2 * HD + 1], 1.0).then_inc(setup, 1)
            pool.wait_ge(setup, 3)
            layernorm_rstd(pool, 0)
            pool.wait_ge(absmax_done, 3)
            nc.gpsimd.partition_all_reduce(wmax_all[:, 0:3], wmax[:, 0:3], P, RMAX).then_inc(absmax_all, 1)
            layernorm_lo(pool, 0)
            pool.wait_ge(wlo_done, 3)
            pool.wait_ge(xl_ready, T)
            nc.gpsimd.memset(stk[STK:ROWS, H:HA, :], -float(2 ** MAX_DOWN)).then_inc(setup, 1)
            pool.wait_ge(setup, 4)

            def sum_over_all(n):
                pool.wait_ge(sum_done, n + 1)
                nc.gpsimd.partition_all_reduce(total[:, n:n + 1], part[:, n:n + 1], P, RADD).then_inc(sum_all, 1)

            def below(n, c):
                part_ = slice(c * E, (c + 1) * E)
                if c == 0:
                    pool.wait_ge(theta_done, 2 * n + 2)
                if n == 2:
                    pool.wait_ge(gate_t, C)
                nc.gpsimd.tensor_scalar(flat[n][:, part_], raws[n][:, part_], ntheta[:, n:n + 1], None,
                                        ALU.is_lt).then_inc(neg_done, 1)

            sum_over_all(0)
            rope_lo(pool, 0, lambda t: below(0, t))
            pool.wait_ge(absmax_done, 4)
            nc.gpsimd.partition_all_reduce(wmax_all[:, 3:4], wmax[:, 3:4], P, RMAX).then_inc(absmax_all, 1)
            for n in (1, 2):
                sum_over_all(n)
                for c in range(C):
                    below(n, c)
            all_pairs(pool, 0, pair_pool)
            last_head_pool(pool, 0)
            with pool.Fori(1, B) as b:
                layernorm_lo(pool, b)
                rope_lo(pool, b)
                all_pairs(pool, b, pair_pool)
                last_head_pool(pool, b)

        def weight_parts():
            return [(w_raw[:, :, lo:lo + n], (w_qkv[:, 0, :, lo:lo + n], w_qkv[:, 1, :, lo:lo + n]))
                    for lo, n in ((0, 512), (512, 256), (768, 256))] + [
                        (wo_raw, (w_o[:, 0], w_o[:, 1]))]

        def attn_t_act(act, b, t):
            act.wait_ge(aT_ready, (b - 1) * T + t + 1)
            if t == 0:
                act.wait_ge(hid_done, b * 2 * H)
            nc.scalar.copy(a_t[:, :, :, t * P:(t + 1) * P].rearrange("p s c n -> p (s c) n"),
                           bank16(4 + t % 2).rearrange("p (k n) -> p k n", n=P)).then_inc(attnT_ready, 1)

        def front_act(act, b, sums_too=None):
            first = isinstance(b, int)

            def hi_part(t):
                act.wait_ge(xs_ready, b * T + t + 1)
                if t >= 2:
                    act.wait_ge(xT_ready, b * T + t - 1)
                elif t == 0:
                    ge(act, pv_done, b * H)
                nc.scalar.copy(x_tok[:, t % 2, 0, :], xs32[:, t % 2, :]).then_inc(xh_ready, 1)

            def xn_out(t):
                act.wait_ge(xT_ready, b * T + t + 1)
                nc.scalar.copy(xn_t[:, :, :, t * P:(t + 1) * P].rearrange("p s c n -> p (s c) n"),
                               bank16(5 - t % 2).rearrange("p (k n) -> p k n", n=P)).then_inc(xnT_ready, 1)

            hi_part(0)
            hi_part(1)
            xn_out(0)
            hi_part(2)
            xn_out(1)
            hi_part(3)
            xn_out(2)
            xn_out(3)
            for c in range(C):
                if sums_too:
                    sums_too(0, c)
            for t in range(T):
                act.wait_ge(r32_ready, b * T + t + 1)
                ge(act, qkT_ready, b * 3 * T + 3 * (t - 1))
                stack = tk[t % 2]
                nc.scalar.copy(stack[:, :, HD:2 * HD], r32)
                nc.scalar.copy(stack[:, 0:H, 0:HD], r32[:, 0:H, :])
                nc.scalar.copy(stack[:, H:HA, 2 * HD:3 * HD], r32[:, H:HA, :]).then_inc(rhi_done, 1)
                if t == 0 and not first:
                    for u in range(T):
                        attn_t_act(act, b, u)
                for g in range(3):
                    k = 3 * t + g
                    act.wait_ge(qkT_ready, b * 3 * T + k + 1)
                    nc.scalar.copy(stk[0:STK, 8 * g:8 * g + 8, t * P:(t + 1) * P],
                                   bank16(4 + k % 2)[0:STK, :].rearrange("p (h n) -> p h n", n=P)
                                   ).then_inc(stack_done, 1)
                if sums_too:
                    sums_too(1, t)

        def maxima_act(act, b):
            act.wait_ge(mT_ready, b + 1)
            ge(act, m_rows, b * 32)
            nc.scalar.copy(m_row[:], bank16(0)[0:2 * H, 0:S]).then_inc(m_row_s, 1)

        def head_act(act, n, j):
            for half in range(2):
                act.wait_ge(sc_ready, 2 * n + half + 1)
                scores = psum[:, 2 * half:2 * half + 2, :]
                ge(act, pl_ready, 2 * n + half - 1)
                nc.scalar.activation(p32[:, half, :], scores, ACT.Exp, scale=SC).then_inc(p32_ready, 1)
                if half == 0:
                    ge(act, pv_done, n - 1)
                nc.scalar.activation(ph[:, j, 2 * half:2 * half + 2, :], scores, ACT.Exp,
                                     scale=SC).then_inc(exp_done, 1)
                if half == 0:
                    act.wait_ge(up_ready, n + 1)
                    ge(act, t1_done, n - 1)
                    nc.scalar.activation(th[:, j, :], psum[:, BU, :], ACT.Tanh,
                                         scale=TANH).then_inc(tanh_done, 1)

        def pair_act(b, i):
            act = nc.scalar
            n = (b * (H // 2) + i) * 2
            if isinstance(i, int) and isinstance(b, int):
                act.wait_ge(coef_done, 1)
            head_act(act, n, 0)
            head_act(act, n + 1, 1)

        @block.scalar
        def _(act):
            def hi_weights(n):
                src, dst = weight_parts()[n]
                nc.scalar.activation(dst[0], src, ACT.Copy, scale=winv[:, n:n + 1]).then_inc(whi_done, 1)

            def absolute_sums(n, c):
                act.wait_ge(arrived[n][c], 16)
                for k in (2 * c, 2 * c + 1):
                    ge(act, sum_part, 2 * C * n + k)
                    nc.scalar.activation(psum[:, 6:8, :], raws[n][:, k * E // 2:(k + 1) * E // 2], ACT.Abs,
                                         accum_out=sums[:, n, k:k + 1]).then_inc(sum_part, 1)

            act.wait_ge(winv_done, 1)
            for n in range(3):
                hi_weights(n)
            front_act(act, 0, absolute_sums)
            act.wait_ge(winv_done, 2)
            hi_weights(3)
            for c in range(C):
                absolute_sums(2, c)
            maxima_act(act, 0)
            all_pairs(act, 0, pair_act)
            with act.Fori(1, B) as b:
                front_act(act, b)
                maxima_act(act, b)
                all_pairs(act, b, pair_act)
            for t in range(T):
                attn_t_act(act, B, t)

        def layernorm_stats(dve, b):
            dve.wait_ge(x_in_s, 16 * (b + 1))
            for t in range(T):
                nc.vector.bn_stats(stats[:, t, :], x_in[:, t, :]).then_inc(mv_done, 1)
            dve.wait_ge(mv_done, b * (2 * T) + T)
            nc.vector.memset(spare[:], 0.0)
            for t in range(T):
                nc.vector.bn_aggr(mv[:, t, :], stats[:, t, :]).then_inc(mv_done, 1)
            dve.wait_ge(mv_done, (b + 1) * (2 * T))
            nc.vector.tensor_scalar(rstd[:, 0, :], mv[:, :, 1], EPS, None, ALU.add).then_inc(eps_done, 1)

        def layernorm_scale(dve, b):
            dve.wait_ge(pow_done, b + 1)
            v, r, a, c, f = (rstd[:, k, :] for k in range(5))
            nc.vector.tensor_tensor(a, r, r, ALU.mult).then_inc(newton, 1)
            dve.wait_ge(newton, 3 * b + 1)
            nc.vector.tensor_tensor(c, a, v, ALU.mult).then_inc(newton, 1)
            dve.wait_ge(newton, 3 * b + 2)
            nc.vector.tensor_scalar(f, c, -0.5 * 2.0 ** X_UP, 1.5 * 2.0 ** X_UP, ALU.mult,
                                    ALU.add).then_inc(newton, 1)
            dve.wait_ge(newton, 3 * b + 3)
            nc.vector.tensor_tensor(rstd[:, 5, :], f, r, ALU.mult).then_inc(rstd_done, 1)

        def layernorm_apply(dve, b, t):
            if t == 0:
                dve.wait_ge(rstd_done, b + 1)
                ge(dve, pv_done, b * H - 1)
            if t >= 2:
                dve.wait_ge(xl_ready, b * T + t - 1)
            nc.vector.tensor_scalar(xs32[:, t % 2, :], x_in[:, t, :], mv[:, t, 0:1], rstd[:, 5, t:t + 1],
                                    ALU.subtract, ALU.mult).then_inc(xs_ready, 1)

        def qk_dve(dve, b, between=lambda t: None):
            if isinstance(b, int):
                dve.wait_ge(const_in, 48)
            for t in range(T):
                n = b * T + t
                dve.wait_ge(qkv_ready, n + 1)
                q = psum[:, 2 * (t % 2), :].rearrange("p (h d) -> p h d", d=HD)
                kv = psum[:, 2 * (t % 2) + 1, :]
                k = kv[:, 0:KV * HD].rearrange("p (h d) -> p h d", d=HD)
                v = kv[:, KV * HD:].rearrange("p (h d) -> p h d", d=HD)
                if t == 0 and not isinstance(b, int):
                    dve.wait_ge(pl_ready, b * 2 * H)
                ge(dve, r32_ready, n)
                for src, h0, h1 in ((q, 0, H), (k, H, HA)):
                    for dst, tab in ((rope_a, cos_t), (rope_b, sin_t)):
                        nc.vector.tensor_tensor(dst[:, h0:h1, :], src,
                                                tab[:, t:t + 1, :].to_broadcast([P, h1 - h0, HD]),
                                                ALU.mult).then_inc(rope_step, 1)
                vh, vl = v_all[:, t, :, 0:HD], v_all[:, t, :, HD:2 * HD]
                down = 2.0 ** -(X_UP + W_UP)
                nc.vector.tensor_scalar(vh, v, down, None, ALU.mult).then_inc(vh_done, 1)
                dve.wait_ge(vh_done, n + 1)
                nc.vector.scalar_tensor_tensor(vl, v, down, vh, ALU.mult, ALU.subtract).then_inc(qkv_used, 1)
                dve.wait_ge(rope_step, 4 * (n + 1))
                ge(dve, rlo_done, n)
                even, odd = slice(0, HD, 2), slice(1, HD, 2)
                nc.vector.tensor_tensor(r32[:, :, even], rope_a[:, :, even], rope_b[:, :, odd], ALU.add)
                nc.vector.tensor_tensor(r32[:, :, odd], rope_a[:, :, odd], rope_b[:, :, even],
                                        ALU.add).then_inc(r32_ready, 1)
                between(t)

        def maxima_dve(dve, b, between):
            for g in range(MAX_GROUPS):
                h, pair = g // 2, g % 2
                dve.wait_ge(mx_ready, b * MAX_GROUPS + g + 1)
                nc.vector.tensor_reduce(mx[:, 2 * pair:2 * pair + 2, h],
                                        psum[:, 2 * (g % 2):2 * (g % 2) + 2, :], AX.X,
                                        ALU.max).then_inc(mx_done, 1)
                if g in between:
                    between[g]()
            down = 2.0 ** -MAX_DOWN
            dve.wait_ge(mx_done, (b + 1) * MAX_GROUPS)
            nc.vector.tensor_scalar(m_tok[:, :, 0, :], mx[:], down, None, ALU.mult).then_inc(mh_done, 1)
            dve.wait_ge(mh_done, b + 1)
            nc.vector.scalar_tensor_tensor(m_tok[:, :, 1, :], mx[:], down, m_tok[:, :, 0, :], ALU.mult,
                                           ALU.subtract).then_inc(ml_done, 1)

        def y_after(dve, b):
            return {5: lambda: y_down(dve, b, 2), 14: lambda: y_down(dve, b, 3),
                    18: lambda: y_attn(dve, b, 0), 22: lambda: y_attn(dve, b, 1),
                    28: lambda: y_attn(dve, b, 2), 31: lambda: y_attn(dve, b, 3)}

        def y_down(dve, b, t):
            n = (b - 1) * T + t
            dve.wait_ge(down_ready, n + 1)
            nc.vector.scalar_tensor_tensor(y[:, t, :], psum[:, DOWN_BANK[t], :], CD, y[:, t, :], ALU.mult,
                                           ALU.add).then_inc(y1_done, 1)

        def y_attn(dve, b, t):
            n = (b - 1) * T + t
            dve.wait_ge(wo_ready, n + 1)
            dve.wait_ge(y1_done, n + 1)
            nc.vector.scalar_tensor_tensor(y[:, t, :], psum[:, WO_BANK[t], :], CA, y[:, t, :], ALU.mult,
                                           ALU.add).then_inc(y_ready, 1)

        def normalise(dve, n, j):
            dve.wait_ge(pv_done, n + 1)
            o = psum[:, 6 + j, 0:T * (2 * HD + 1)].rearrange("p (t d) -> p t d", t=T)
            ge(dve, ef_done, n)
            nc.vector.reciprocal(rden[:], o[:, :, 2 * HD:2 * HD + 1]).then_inc(rden_done, 1)
            dve.wait_ge(rden_done, n + 1)
            ge(dve, attn_done, 2 * (n - 1))
            r = rden[:].to_broadcast([P, T, HD])
            nc.vector.tensor_tensor(norm_e[:, j], o[:, :, 0:HD], r, ALU.mult).then_inc(e_done, 1)
            dve.wait_ge(e_done, n + 1)
            nc.vector.tensor_tensor(norm_f[:, j], o[:, :, HD:2 * HD], r, ALU.mult).then_inc(ef_done, 1)

        def head_dve(dve, n, j, first):
            def lo_part(half):
                dve.wait_ge(exp_done, 2 * n + half + 1)
                if half == 0:
                    ge(dve, pv_done, n - 1)
                nc.vector.tensor_tensor(pl[:, j, 2 * half:2 * half + 2, :].rearrange("p a b -> p (a b)"),
                                        p32[:, half, :],
                                        ph[:, j, 2 * half:2 * half + 2, :].rearrange("p a b -> p (a b)"),
                                        ALU.subtract).then_inc(pl_ready, 1)

            lo_part(0)
            dve.wait_ge(tanh_done, n + 1)
            ge(dve, h32_ready, n)
            nc.vector.scalar_tensor_tensor(t1, th[:, j, :], 1.0, psum[:, BU, :], ALU.add,
                                           ALU.mult).then_inc(t1_done, 1)
            dve.wait_ge(t1_done, n + 1)
            dve.wait_ge(gate_ready, n + 1)
            ge(dve, hid_done, 2 * (n - 1))
            nc.vector.scalar_tensor_tensor(h32[:, j, :], t1, 2.0 ** -(H_DOWN + 2 * X_UP), psum[:, BG, :],
                                           ALU.mult, ALU.mult).then_inc(h32_ready, 1)
            lo_part(1)
            if not first:
                normalise(dve, n - 1, 1 - j)

        def pair_dve(b, i):
            dve = nc.vector
            n = (b * (H // 2) + i) * 2
            head_dve(dve, n, 0, isinstance(i, int))
            if isinstance(i, int):
                layernorm_stats(dve, b + 1)
            head_dve(dve, n + 1, 1, False)
            if isinstance(i, int):
                layernorm_scale(dve, b + 1)

        def last_head_dve(dve, b):
            normalise(dve, b * H + H - 1, 1)

        @block.vector
        def _(dve):
            def largest(n, s_in):
                dve.wait_ge(s_in, 16)
                nc.vector.tensor_reduce(wmax[:, n:n + 1], weight_parts()[n][0], AX.XY, ALU.max,
                                        apply_absolute_value=True).then_inc(absmax_done, 1)

            def exponents(lo, hi, k):
                some = slice(lo, hi)
                dve.wait_ge(absmax_all, k + 1)
                nc.vector.tensor_scalar(wmax_all[:, some], wmax_all[:, some], 2.0 ** -100, 2.0 ** 100,
                                        ALU.max, ALU.min).then_inc(winv_step, 1)
                dve.wait_ge(winv_step, 3 * k + 1)
                nc.vector.tensor_scalar(wpow[:, some].bitcast(U32), wmax_all[:, some].bitcast(U32),
                                        0x7F800000, None, ALU.bitwise_and).then_inc(winv_step, 1)
                dve.wait_ge(winv_step, 3 * k + 2)
                nc.vector.reciprocal(winv[:, some], wpow[:, some]).then_inc(winv_step, 1)
                dve.wait_ge(winv_step, 3 * k + 3)
                nc.vector.tensor_scalar(winv[:, some], winv[:, some], 2.0 ** W_UP, None,
                                        ALU.mult).then_inc(winv_done, 1)
                dve.wait_ge(winv_done, k + 1)

            def lo_weights(n):
                src, dst = weight_parts()[n]
                dve.wait_ge(whi_done, n + 1)
                nc.vector.scalar_tensor_tensor(dst[1], src, winv[:, n:n + 1], dst[0], ALU.mult,
                                               ALU.subtract).then_inc(wlo_done, 1)

            def thresholds(n):
                dve.wait_ge(sum_part, 2 * C * (n + 1))
                nc.vector.tensor_reduce(part[:, n:n + 1], sums[:, n, :], AX.X, ALU.add).then_inc(sum_done, 1)
                dve.wait_ge(sum_all, n + 1)
                nc.vector.tensor_scalar(scale[:, n:n + 1], total[:, n:n + 1], 1.0 / (E * D), 1e-8, ALU.mult,
                                        ALU.add).then_inc(theta_done, 1)
                dve.wait_ge(theta_done, 2 * n + 1)
                nc.vector.tensor_scalar(theta[:, n:n + 1], scale[:, n:n + 1], 0.5, None, ALU.mult)
                nc.vector.tensor_scalar(ntheta[:, n:n + 1], scale[:, n:n + 1], -0.5, None,
                                        ALU.mult).then_inc(theta_done, 1)
                dve.wait_ge(theta_done, 2 * n + 2)

            def ternary(n, c):
                part_ = slice(c * E, (c + 1) * E)
                dve.wait_ge(neg_done, C * n + c + 1)
                nc.vector.scalar_tensor_tensor(flat[n][:, part_], raws[n][:, part_], theta[:, n:n + 1],
                                               flat[n][:, part_], ALU.is_gt,
                                               ALU.subtract).then_inc(turned[n], 1)

            def coefficients():
                def step(out_, a, b_):
                    nonlocal k
                    nc.vector.tensor_tensor(out_, a, b_, ALU.mult).then_inc(coef_step, 1)
                    k += 1
                    dve.wait_ge(coef_step, k)
                k = 0
                step(coef[:, 4:5], wpow[:, WQ:WQ + 1], wpow[:, WK:WK + 1])
                step(coef[:, 5:6], wpow[:, WV:WV + 1], wpow[:, WO:WO + 1])
                step(coef[:, 6:7], scale[:, 0:1], scale[:, 1:2])
                step(coef[:, 7:8], coef[:, 6:7], scale[:, 2:3])
                nc.vector.tensor_scalar(SC, coef[:, 4:5], float(HD) ** -0.5, None, ALU.mult)
                nc.vector.tensor_scalar(TANH, scale[:, 0:1], 0.5 * 2.0 ** -X_UP, None, ALU.mult)
                nc.vector.tensor_scalar(CD, coef[:, 7:8], 2.0 ** (H_DOWN - 1), None, ALU.mult)
                nc.vector.tensor_scalar(CA, coef[:, 5:6], 2.0 ** -W_UP, None, ALU.mult).then_inc(coef_done, 1)

            layernorm_stats(dve, 0)
            for n, s_in in enumerate((wq_in, wk_in, wv_in)):
                largest(n, s_in)
            exponents(0, 3, 0)
            layernorm_scale(dve, 0)
            layernorm_apply(dve, 0, 0)
            layernorm_apply(dve, 0, 1)
            for n in range(3):
                lo_weights(n)
            layernorm_apply(dve, 0, 2)
            layernorm_apply(dve, 0, 3)
            thresholds(0)
            qk_dve(dve, 0, lambda t: ternary(0, t))
            largest(3, wo_in)
            thresholds(1)
            exponents(3, 4, 1)
            for c in range(C):
                ternary(1, c)
            maxima_dve(dve, 0, {10: lambda: lo_weights(3), 20: lambda: thresholds(2)})
            for c in range(C):
                ternary(2, c)
            coefficients()
            all_pairs(dve, 0, pair_dve)
            with dve.Fori(1, B) as b:
                layernorm_apply(dve, b, 0)
                layernorm_apply(dve, b, 1)
                last_head_dve(dve, b - 1)
                dve.wait_ge(y_in, 16 * b)
                y_down(dve, b, 0)
                layernorm_apply(dve, b, 2)
                layernorm_apply(dve, b, 3)
                qk_dve(dve, b)
                y_down(dve, b, 1)
                maxima_dve(dve, b, y_after(dve, b))
                all_pairs(dve, b, pair_dve)
            last_head_dve(dve, B - 1)
            dve.wait_ge(y_in, 16 * B)
            for t in range(T):
                y_down(dve, B, t)
            for t in range(T):
                y_attn(dve, B, t)

        def pe_front(pe, b):
            first = isinstance(b, int)

            def transpose8(bank, src, inc):
                for k in range(8):
                    m = nc.tensor.transpose(bank16(bank)[:, k * P:(k + 1) * P], src(k), ident[:])
                m.then_inc(inc, 1)

            def x_t(t):
                pe.wait_ge(xl_ready, b * T + t + 1)
                if t >= 2:
                    pe.wait_ge(xnT_ready, b * T + t - 1)
                elif t == 0:
                    ge(pe, h32_ready, b * H)
                elif not first:
                    pe.wait_ge(y1_done, (b - 1) * T + 1)
                transpose8(5 - t % 2, lambda k: x_tok[:, t % 2, k // C, (k % C) * P:(k % C + 1) * P],
                           xT_ready)

            def qkv(t):
                pe.wait_ge(xnT_ready, b * T + t + 1)
                if t == 0:
                    ge(pe, exp_done, b * 2 * H)
                if t >= 2:
                    pe.wait_ge(qkv_used, b * T + t - 1)
                bank = 2 * (t % 2)
                for side in range(2):
                    k = 0
                    for c in range(C):
                        for xp, wp in ((0, 0), (0, 1), (1, 0)):
                            m = nc.tensor.matmul(psum[:, bank + side, :], xn_t[:, xp, c, t * P:(t + 1) * P],
                                                 w_qkv[:, wp, c, side * 512:side * 512 + 512],
                                                 start=k == 0, stop=k == 3 * C - 1)
                            k += 1
                m.then_inc(qkv_ready, 1)

            def qk_t(t):
                pe.wait_ge(rlo_done, b * T + t + 1)
                for g in range(3):
                    k = 3 * t + g
                    if k >= 2:
                        pe.wait_ge(stack_done, b * 3 * T + k - 1)
                    elif first:
                        pe.wait_ge(xnT_ready, T)
                    else:
                        pe.wait_ge(attnT_ready, b * T)
                    for h in range(8):
                        m = nc.tensor.transpose(bank16(4 + k % 2)[0:STK, h * P:(h + 1) * P],
                                                tk[t % 2][:, 8 * g + h, :], ident[:])
                    m.then_inc(qkT_ready, 1)

            def maxima(g):
                h, pair = g // 2, g % 2
                if g >= 2:
                    pe.wait_ge(mx_done, b * MAX_GROUPS + g - 1)
                for u in range(2):
                    t = 2 * pair + u
                    m = nc.tensor.matmul(psum[:, 2 * (g % 2) + u, :], stk[0:STK, h, t * P:(t + 1) * P],
                                         stk[0:STK, H + h // 2, :], start=True, stop=True)
                m.then_inc(mx_ready, 1)

            if first:
                pe.wait_ge(const_in, 48)
                for t in range(T):
                    x_t(t)
                pe.wait_ge(wlo_done, 3)
                for t in range(2):
                    qkv(t)
                qk_t(0)
                qkv(2)
                qk_t(1)
                qkv(3)
                qk_t(2)
                qk_t(3)
                tail = []
            else:
                run_tail(pe, down_steps(pe, b, 0)[PE_EARLY:])
                x_t(0)
                tail = [f for t in (1, 2, 3) for f in down_steps(pe, b, t)]
                tail += [f for t in range(T) for f in wo_steps(pe, b, t)]

                def some(n):
                    run_tail(pe, tail[:n])
                    del tail[:n]

                some(12)
                x_t(1)
                some(4)
                x_t(2)
                some(4)
                x_t(3)
                some(4)
                qkv(0)
                attn_t_pe(pe, b, 0)
                attn_t_pe(pe, b, 1)
                qkv(1)
                attn_t_pe(pe, b, 2)
                attn_t_pe(pe, b, 3)
                qk_t(0)
                qkv(2)
                qk_t(1)
                qkv(3)
                some(8)
                qk_t(2)
                some(20)
                qk_t(3)
                some(8)
            pe.wait_ge(qkv_used, (b + 1) * T)
            pe.wait_ge(stack_done, (b + 1) * 3 * T)
            for g in range(MAX_GROUPS):
                maxima(g)
                lo = len(tail) * g // MAX_GROUPS
                hi = len(tail) * (g + 1) // MAX_GROUPS
                run_tail(pe, tail[lo:hi])
            pe.wait_ge(ml_done, b + 1)
            for t in range(T):
                m = nc.tensor.transpose(bank16(0)[0:2 * H, t * P:(t + 1) * P],
                                        m_tok[:, t, :, :].rearrange("p s h -> p (s h)"), ident[:])
            m.then_inc(mT_ready, 1)

        def run_tail(pe, steps):
            for step in steps:
                step()

        def attn_t_pe(pe, b, t):
            if t == 0:
                pe.wait_ge(attn_done, b * 2 * H)
            if t < 2 and isinstance(b, int):
                pe.wait_ge(h32_ready, B * H)
                pe.wait_ge(y1_done, (B - 1) * T + 1)
            elif t < 2:
                pe.wait_ge(xnT_ready, (b + 1) * T)
            else:
                pe.wait_ge(attnT_ready, (b - 1) * T + t - 1)
            for k in range(8):
                m = nc.tensor.transpose(bank16(4 + t % 2)[:, k * P:(k + 1) * P],
                                        a_tok[:, k // C, t, (k % C) * P:(k % C + 1) * P], ident[:])
            m.then_inc(aT_ready, 1)

        def down_steps(pe, b, t):
            def step(k):
                def go():
                    e, s_ = k // 2, k % 2
                    if t == 0 and k == 0:
                        pe.wait_ge(t1_done, b * H)
                        pe.wait_ge(hid_done, b * 2 * H - 2)
                    if t == 0 and e == ET - 1 and s_ == 0:
                        pe.wait_ge(hid_done, b * 2 * H)
                    if t in (1, 2) and k == 0:
                        pe.wait_ge(ef_done, b * H)
                    if t == 3 and k == 0:
                        pe.wait_ge(y1_done, (b - 1) * T + 2)
                    m = nc.tensor.matmul(psum[:, DOWN_BANK[t], :], hid[:, s_, e, t * P:(t + 1) * P],
                                         t_down[:, e, :], start=k == 0, stop=k == 2 * ET - 1)
                    if k == 2 * ET - 1:
                        m.then_inc(down_ready, 1)
                return go
            return [step(k) for k in range(2 * ET)]

        def wo_steps(pe, b, t):
            def step(k):
                def go():
                    c, (ap, wp) = k // 3, ((0, 0), (0, 1), (1, 0))[k % 3]
                    if k == 0 and t == 0:
                        pe.wait_ge(attnT_ready, b * T)
                    if k == 0 and t < 2:
                        pe.wait_ge(y1_done, (b - 1) * T + t + 3)
                    if k == 0 and t >= 2:
                        pe.wait_ge(y_ready, (b - 1) * T + t - 1)
                    m = nc.tensor.matmul(psum[:, WO_BANK[t], :], a_t[:, ap, c, t * P:(t + 1) * P],
                                         w_o[:, wp, c, :], start=k == 0, stop=k == 3 * C - 1)
                    if k == 3 * C - 1:
                        m.then_inc(wo_ready, 1)
                return go
            return [step(k) for k in range(3 * C)]

        def pe_pv(pe, n, j, g):
            pe.wait_ge(pl_ready, 2 * n + 2)
            ge(pe, ef_done, n - 1)
            for t in range(T):
                for kt in range(T):
                    for s_, p_part in enumerate((ph, pl)):
                        m = nc.tensor.matmul(psum[:, 6 + j, t * (2 * HD + 1):(t + 1) * (2 * HD + 1)],
                                             p_part[:, j, kt, t * P:(t + 1) * P], v_all[:, kt, g, :],
                                             start=kt == 0 and s_ == 0, stop=kt == T - 1 and s_ == 1)
            m.then_inc(pv_done, 1)

        PE_EARLY = 8

        def pe_last(pe, b):
            run_tail(pe, down_steps(pe, b, 0)[:PE_EARLY])
            pe_pv(pe, b * H - 1, 1, KV - 1)

        def scores_pe(pe, b, n, h, i, first):
            for half in range(2):
                if not first:
                    pe.wait_ge(exp_done, 2 * (n - 1) + half + 1)
                elif half == 0:
                    pe.wait_ge(m_row_s, b + 1)
                    pe.wait_ge(m_rows, 32 * (b + 1))
                for u in range(2):
                    kt = 2 * half + u
                    m = nc.tensor.matmul(psum[:, kt, :], stk[0:ROWS, H + i, kt * P:(kt + 1) * P],
                                         stk[0:ROWS, h, :], start=True, stop=True)
                m.then_inc(sc_ready, 1)

        def up_gate_pe(pe, n, h):
            for w, bank, done in ((t_up, BU, up_ready), (t_gate, BG, gate_ready)):
                if bank == BU:
                    ge(pe, t1_done, n)
                else:
                    ge(pe, h32_ready, n)
                for c in range(C):
                    for s_ in range(2):
                        m = nc.tensor.matmul(psum[:, bank, :], w[:, c, bass.ts(h, P)], xn_t[:, s_, c, :],
                                             start=c == 0 and s_ == 0, stop=c == C - 1 and s_ == 1)
                m.then_inc(done, 1)

        def pair_pe(b, i):
            pe = nc.tensor
            n = (b * (H // 2) + i) * 2
            start = isinstance(i, int)
            if start:
                if isinstance(b, int):
                    pe.wait_ge(up_t, C)
                    pe.wait_ge(gate_t, C)
                    pe.wait_ge(setup, 4)
                up_gate_pe(pe, n, i * 2)
                scores_pe(pe, b, n, i * 2, i, True)
            else:
                scores_pe(pe, b, n, i * 2, i, False)
                up_gate_pe(pe, n, i * 2)
                pe_pv(pe, n - 1, 1, i - 1)
            scores_pe(pe, b, n + 1, i * 2 + 1, i, False)
            up_gate_pe(pe, n + 1, i * 2 + 1)
            if start:
                ge(pe, y_ready, b * T)
            pe_pv(pe, n, 0, i)

        @block.tensor
        def _(pe):
            pe_front(pe, 0)
            all_pairs(pe, 0, pair_pe)
            pe.wait_ge(down_t, C)
            pe_last(pe, 1)
            with pe.Fori(1, B) as b:
                pe_front(pe, b)
                all_pairs(pe, b, pair_pe)
                pe_last(pe, b + 1)
            run_tail(pe, down_steps(pe, B, 0)[PE_EARLY:])
            run_tail(pe, down_steps(pe, B, 1))
            for t in range(T):
                attn_t_pe(pe, B, t)
            for t in (2, 3):
                run_tail(pe, down_steps(pe, B, t))
            for t in range(T):
                run_tail(pe, wo_steps(pe, B, t))


def rope_tables():
    inv_freq = (1.0 / np.float32(10000.0) ** (np.arange(0, HD, 2, dtype=np.float32) / np.float32(HD))).astype(np.float32)
    angle = (np.arange(S, dtype=np.float32)[:, None] * inv_freq[None, :]).astype(np.float32)
    down = np.float32(2.0 ** -(X_UP + W_UP))
    cos, sin = np.cos(angle) * down, np.sin(angle) * down
    c = np.repeat(cos, 2, axis=1).astype(np.float32)
    sn = np.stack([sin, -sin], axis=2).reshape(S, HD).astype(np.float32)
    return c, sn


def kernel(L0_attn_x, L0_attn_wq, L0_attn_wk, L0_attn_wv, L0_attn_wo, L0_ffn_W_up, L0_ffn_W_gate, L0_ffn_W_down):
    import concourse.bacc as bacc
    from concourse.bass_utils import run_bass_kernel_spmd

    c, sn = rope_tables()
    arrays = {
        "x": L0_attn_x, "wq": L0_attn_wq, "wk": L0_attn_wk, "wv": L0_attn_wv, "wo": L0_attn_wo,
        "w_up_t": np.asarray(L0_ffn_W_up).T, "w_gate_t": np.asarray(L0_ffn_W_gate).T,
        "w_down_t": np.asarray(L0_ffn_W_down).T,
        "rope_c": c, "rope_s": sn, "ident": np.eye(P, dtype=np.float16),
    }
    arrays = {k: np.ascontiguousarray(v) for k, v in arrays.items()}
    nc = bacc.Bacc("TRN2", target_bir_lowering=False, num_devices=1)
    aps = [nc.dram_tensor(k, v.shape, mybir.dt.from_np(v.dtype), kind="ExternalInput").ap()
           for k, v in arrays.items()]
    out = nc.dram_tensor("out", (B, S, D), F32, kind="ExternalOutput").ap()
    build(nc, *aps, out)
    r = run_bass_kernel_spmd(nc, [arrays], core_ids=[0])
    return r.results[0]["out"]
```

```python
import concourse.bass as bass
from concourse import mybir
from contextlib import ExitStack
import numpy as np

F32 = mybir.dt.float32
F16 = mybir.dt.float16
U32 = mybir.dt.uint32
ALU = mybir.AluOpType
ACT = mybir.ActivationFunctionType
AX = mybir.AxisListType
RMAX = bass.bass_isa.ReduceOp.max
RADD = bass.bass_isa.ReduceOp.add

P = 128
B, S, D = 4, 512, 512
H, KV, HD = 16, 8, 32
HA = H + KV
E = 2048
C = D // P
T = S // P
ET = E // P
STK = 3 * HD
ROWS = STK + 2
EPS = 1e-5

X_UP = 11
W_UP = 14
MAX_DOWN = 9
H_DOWN = 4
MAX_GROUPS = T * KV


def build(nc, x, wq, wk, wv, wo, w_up_t, w_gate_t, w_down_t, rope_c, rope_s, ident_in, out):
    ctx = ExitStack()
    with ctx:
        def sb(name, shape, dt):
            return ctx.enter_context(nc.sbuf_tensor(name, shape, dt))

        def sem(name):
            return ctx.enter_context(nc.semaphore(name))

        def as16(ap):
            return ap.bitcast(F16)

        x_v = x.rearrange("b (t p) d -> b p t d", p=P)
        out_v = out.rearrange("b (t p) d -> b p t d", p=P)

        t_up = sb("t_up", [P, C, E], F16)
        t_gate = sb("t_gate", [P, C, E], F16)
        w_qkv = sb("w_qkv", [P, 2, C, 1024], F16)
        w_o = sb("w_o", [P, 2, C, D], F16)
        ident = sb("identity", [P, P], F16)
        cos_t = sb("cos_t", [P, T, HD], F32)
        sin_t = sb("sin_t", [P, T, HD], F32)
        v_all = sb("v_all", [P, T, KV, 2 * HD + 1], F16)
        xn_t = sb("xn_t", [P, 2, C, S], F16)
        x_in = sb("x_in", [P, T, D], F32)

        late = sb("late", [P, 8192], F32)
        t_down = as16(late[:, 0:4096]).rearrange("p (e d) -> p e d", e=ET)
        a_tok = as16(late[:, 4096:6144]).rearrange("p (s t d) -> p s t d", s=2, t=T)
        y = late[:, 6144:8192].rearrange("p (t d) -> p t d", t=T)

        hid_raw = sb("hid_raw", [P, 8192], F32)
        hid = as16(hid_raw[:, :]).rearrange("p (s e n) -> p s e n", s=2, e=ET)

        stk_raw = sb("stk_raw", [P, 6144], F32)
        stk = as16(stk_raw[:, :]).rearrange("p (h n) -> p h n", h=HA)
        w_raw = stk_raw[:, 0:4096].rearrange("p (c n) -> p c n", c=C)

        p32 = sb("p32", [P, 2, 2 * S], F32)
        ph = sb("ph", [P, 2, T, S], F16)
        pl = sb("pl", [P, 2, T, S], F16)
        rope_a = p32[:, 0, 0:HA * HD].rearrange("p (h d) -> p h d", d=HD)
        rope_b = p32[:, 1, 0:HA * HD].rearrange("p (h d) -> p h d", d=HD)
        xs32 = ph[:, 0, :, :].rearrange("p a b -> p (a b)").bitcast(F32).rearrange(
            "p (n d) -> p n d", n=2)
        x_tok = ph[:, 1, :, :].rearrange("p a (s d) -> p (a s) d", s=1).rearrange(
            "p (n s) d -> p n s d", n=2)
        pl_flat = pl[:, :, :, :].rearrange("p a b c -> p (a b c)")
        r32 = pl_flat[:, 0:2 * HA * HD].bitcast(F32).rearrange("p (h d) -> p h d", d=HD)
        tk = (pl_flat[:, 2 * HA * HD:2 * HA * HD + HA * STK].rearrange("p (h d) -> p h d", d=STK),
              ph[:, :, :, :].rearrange("p a b c -> p (a b c)")[:, 0:HA * STK].rearrange(
                  "p (h d) -> p h d", d=STK))

        act_raw = sb("act_raw", [P, 5, D], F32)
        th = act_raw[:, 0:2, :]
        t1 = act_raw[:, 2, :]
        h32 = act_raw[:, 3:5, :]
        a_t = act_raw[:, 0:4, :].rearrange("p a b -> p (a b)").bitcast(F16).rearrange(
            "p (s c n) -> p s c n", s=2, c=C)
        wo_raw = act_raw[:, 0:4, :]

        norm_e = sb("norm_e", [P, 2, T, HD], F32)
        norm_f = sb("norm_f", [P, 2, T, HD], F32)
        norm_a = sb("norm_a", [P, T, HD], F32)
        rden = sb("rden", [P, T, 1], F32)
        mx = sb("mx", [P, T, H], F32)
        m_tok = sb("m_tok", [P, T, 2, H], F16)
        m_row = sb("m_row", [2 * H, S], F16)
        stats = sb("stats", [P, T, 6], F32)
        mv = sb("mv", [P, T, 2], F32)
        rstd = sb("rstd", [P, 6, T], F32)
        sums = sb("sums", [P, 3, 2 * C], F32)
        part = sb("part", [P, 3], F32)
        total = sb("total", [P, 3], F32)
        scale = sb("scale", [P, 3], F32)
        theta = sb("theta", [P, 3], F32)
        ntheta = sb("ntheta", [P, 3], F32)
        wmax = sb("wmax", [P, 4], F32)
        wmax_all = sb("wmax_all", [P, 4], F32)
        wpow = sb("wpow", [P, 4], F32)
        winv = sb("winv", [P, 4], F32)
        coef = sb("coef", [P, 8], F32)
        one = sb("one", [P, 1], F32)
        spare = sb("spare", [P, 1], F32)
        minus_half = sb("minus_half", [P, T], F32)
        SC, TANH, CD, CA = (coef[:, n:n + 1] for n in (0, 1, 2, 3))
        WQ, WK, WV, WO = range(4)

        psum = ctx.enter_context(nc.psum_tensor("psum", [P, 8, 512], F32))
        BU, BG = 4, 5
        DOWN_BANK, WO_BANK = (4, 7, 6, 7), (6, 7, 6, 7)

        def bank16(n):
            return psum[:, n, :].bitcast(F16)

        names = """const_in wq_in wk_in wv_in wo_in x_in_s y_in y_out
            absmax_done absmax_all winv_done whi_done wlo_done
            sum_part sum_done sum_all theta_done neg_done up_t gate_t down_t coef_done setup
            mv_done eps_done pow_done newton rstd_done xs_ready xh_ready xl_ready xT_ready xnT_ready
            kv_ready k_step vh_done kv_used kr_ready khi_done klo_done kT_ready kstack_done
            q_ready q_step qr_ready qhi_done qlo_done qT_ready qstack_done
            mx_ready mx_done mh_done ml_done mT_ready m_row_s m_rows
            sc_ready p32_ready exp_done pl_ready pv_done
            up_ready gate_ready tanh_done t1_done h32_ready hid_done
            rden_done e_done ef_done attn_done
            aT_ready attnT_ready down_ready wo_ready y1_done y_ready""".split()
        s = {n: sem(n) for n in names}
        (const_in, wq_in, wk_in, wv_in, wo_in, x_in_s, y_in, y_out,
         absmax_done, absmax_all, winv_done, whi_done, wlo_done,
         sum_part, sum_done, sum_all, theta_done, neg_done, up_t, gate_t, down_t, coef_done, setup,
         mv_done, eps_done, pow_done, newton, rstd_done, xs_ready, xh_ready, xl_ready, xT_ready,
         xnT_ready,
         kv_ready, k_step, vh_done, kv_used, kr_ready, khi_done, klo_done, kT_ready, kstack_done,
         q_ready, q_step, qr_ready, qhi_done, qlo_done, qT_ready, qstack_done,
         mx_ready, mx_done, mh_done, ml_done, mT_ready, m_row_s, m_rows,
         sc_ready, p32_ready, exp_done, pl_ready, pv_done,
         up_ready, gate_ready, tanh_done, t1_done, h32_ready, hid_done,
         rden_done, e_done, ef_done, attn_done,
         aT_ready, attnT_ready, down_ready, wo_ready, y1_done, y_ready) = (s[n] for n in names)

        up_in, gate_in, down_in = ([sem(f"{w}_in{c}") for c in range(C)] for w in ("up", "gate", "down"))
        winv_step, coef_step, more_sum, own_neg = (
            sem(n) for n in ("winv_step", "coef_step", "more_sum", "own_neg"))

        raws = (hid_raw, late, hid_raw)
        flat = (t_up[:, :, :].rearrange("p c e -> p (c e)"), t_gate[:, :, :].rearrange("p c e -> p (c e)"),
                as16(late[:, 0:4096]))
        BELOW_BY_DVE = ((0, 0), (0, 1), (2, 0), (2, 2))
        BELOW_BY_POOL = ((0, 2), (0, 3), (1, 0), (1, 1), (1, 2), (1, 3), (2, 1), (2, 3))
        arrived, turned = (up_in, gate_in, down_in), (up_t, gate_t, down_t)

        block = ctx.enter_context(nc.Block())

        def all_pairs(eng, b, pair):
            pair(b, 0)
            with eng.Fori(1, H // 2) as i:
                pair(b, i)

        def ge(eng, s, value):
            if not isinstance(value, int) or value > 0:
                eng.wait_ge(s, value)

        @block.sync
        def _(sp):
            sp.dma_start(x_in[:], x_v[0]).then_inc(x_in_s, 16)
            for w, s_in, lo, n in ((wq, wq_in, 0, 512), (wk, wk_in, 512, 256), (wv, wv_in, 768, 256)):
                sp.dma_start(w_raw[:, :, lo:lo + n], w.rearrange("(c p) n -> p c n", p=P)).then_inc(s_in, 16)
            sp.dma_start(ident[:], ident_in).then_inc(const_in, 16)
            sp.dma_start(cos_t[:], rope_c.rearrange("(t p) d -> p t d", p=P)).then_inc(const_in, 16)
            sp.dma_start(sin_t[:], rope_s.rearrange("(t p) d -> p t d", p=P)).then_inc(const_in, 16)
            for c in range(C):
                sp.dma_start(hid_raw[:, c * E:(c + 1) * E], w_up_t[c * P:(c + 1) * P, :]).then_inc(up_in[c], 16)
            for c in range(C):
                sp.dma_start(late[:, c * E:(c + 1) * E], w_gate_t[c * P:(c + 1) * P, :]).then_inc(gate_in[c], 16)
            sp.dma_start(wo_raw, wo.rearrange("(c p) n -> p c n", p=P)).then_inc(wo_in, 16)
            sp.wait_ge(xs_ready, T)
            sp.dma_start(x_in[:], x_v[1]).then_inc(x_in_s, 16)
            sp.wait_ge(up_t, C)
            down_v = w_down_t.rearrange("(e p) d -> p e d", p=P)
            hid_v = hid_raw[:, :].rearrange("p (e d) -> p e d", e=ET)
            for c in range(C):
                sp.dma_start(hid_v[:, c * 4:c * 4 + 4, :], down_v[:, c * 4:c * 4 + 4, :]).then_inc(down_in[c], 16)

            def rows_of_maxima(b):
                sp.wait_ge(m_row_s, b + 1)
                for part_ in range(2):
                    sp.dma_start(stk[STK + part_:STK + part_ + 1, 0:H, :],
                                 m_row[part_ * H:(part_ + 1) * H, :]).then_inc(m_rows, 16)

            rows_of_maxima(0)
            with sp.Fori(1, B) as b:
                ge(sp, y_out, (b - 1) * T * 16)
                sp.wait_ge(gate_t, C)
                sp.dma_start(y, x_v[b - 1]).then_inc(y_in, 16)
                sp.wait_ge(xs_ready, (b + 1) * T)
                sp.dma_start(x_in[:], x_v[(b + 1) % B]).then_inc(x_in_s, 16)
                rows_of_maxima(b)
                for t in range(T):
                    sp.wait_ge(y_ready, (b - 1) * T + t + 1)
                    sp.dma_start(out_v[b - 1, :, t, :], y[:, t, :]).then_inc(y_out, 16)
            sp.wait_ge(y_out, (B - 1) * T * 16)
            sp.dma_start(y, x_v[B - 1]).then_inc(y_in, 16)
            for t in range(T):
                sp.wait_ge(y_ready, (B - 1) * T + t + 1)
                sp.dma_start(out_v[B - 1, :, t, :], y[:, t, :]).then_inc(y_out, 16)
            sp.wait_ge(y_out, B * T * 16)

        def layernorm_rstd(pool, b=0):
            pool.wait_ge(eps_done, b + 1)
            nc.gpsimd.tensor_tensor(rstd[:, 1, :], rstd[:, 0, :], minus_half[:], ALU.pow).then_inc(pow_done, 1)

        def layernorm_lo(pool, b):
            for t in range(T):
                pool.wait_ge(xh_ready, b * T + t + 1)
                nc.gpsimd.tensor_tensor(x_tok[:, t % 2, 1, :], xs32[:, t % 2, :], x_tok[:, t % 2, 0, :],
                                        ALU.subtract).then_inc(xl_ready, 1)

        def k_lo(pool, b, t):
            pool.wait_ge(khi_done, b * T + t + 1)
            nc.gpsimd.tensor_tensor(tk[t % 2][:, H:HA, 0:HD], r32[:, H:HA, :], tk[t % 2][:, H:HA, HD:2 * HD],
                                    ALU.subtract).then_inc(klo_done, 1)

        def q_lo(pool, b, t):
            pool.wait_ge(qhi_done, b * T + t + 1)
            nc.gpsimd.tensor_tensor(tk[t % 2][:, 0:H, 2 * HD:3 * HD], r32[:, 0:H, :],
                                    tk[t % 2][:, 0:H, HD:2 * HD], ALU.subtract).then_inc(qlo_done, 1)

        def hidden_pool(pool, n, j, e):
            pool.wait_ge(h32_ready, n + 1)
            nc.gpsimd.tensor_tensor(hid[:, 0, e, :], h32[:, j, :], one[:].to_broadcast([P, D]),
                                    ALU.mult).then_inc(hid_done, 1)
            pool.wait_ge(hid_done, 2 * n + 1)
            nc.gpsimd.tensor_tensor(hid[:, 1, e, :], h32[:, j, :], hid[:, 0, e, :],
                                    ALU.subtract).then_inc(hid_done, 1)

        def attn_pool(pool, n, j, h):
            pool.wait_ge(ef_done, n + 1)
            nc.gpsimd.tensor_tensor(norm_a[:], norm_e[:, j], norm_f[:, j], ALU.add)
            hi = a_tok[:, 0, :, bass.ts(h, HD)]
            lo = a_tok[:, 1, :, bass.ts(h, HD)]
            nc.gpsimd.tensor_tensor(hi, norm_e[:, j], norm_f[:, j], ALU.add).then_inc(attn_done, 1)
            pool.wait_ge(attn_done, 2 * n + 1)
            nc.gpsimd.tensor_tensor(lo, norm_a[:], hi, ALU.subtract).then_inc(attn_done, 1)

        def pair_pool(b, i):
            pool = nc.gpsimd
            n = (b * (H // 2) + i) * 2
            if isinstance(i, int) and i == 0:
                ge(pool, aT_ready, b * T)
            else:
                attn_pool(pool, n - 1, 1, i * 2 - 1)
            hidden_pool(pool, n, 0, i * 2)
            if isinstance(i, int):
                layernorm_rstd(pool, b + 1)
            attn_pool(pool, n, 0, i * 2)
            hidden_pool(pool, n + 1, 1, i * 2 + 1)

        def last_head_pool(pool, b):
            attn_pool(pool, b * H + H - 1, 1, H - 1)

        @block.gpsimd
        def _(pool):
            nc.gpsimd.memset(one[:], 1.0).then_inc(setup, 1)
            nc.gpsimd.memset(minus_half[:], -0.5).then_inc(setup, 1)
            nc.gpsimd.memset(v_all[:, :, :, 2 * HD:2 * HD + 1], 1.0).then_inc(setup, 1)
            pool.wait_ge(setup, 3)
            layernorm_rstd(pool, 0)
            pool.wait_ge(absmax_done, 3)
            nc.gpsimd.partition_all_reduce(wmax_all[:, 0:3], wmax[:, 0:3], P, RMAX).then_inc(absmax_all, 1)
            layernorm_lo(pool, 0)
            pool.wait_ge(wlo_done, 3)
            pool.wait_ge(xl_ready, T)
            nc.gpsimd.memset(stk[STK:ROWS, H:HA, :], -float(2 ** MAX_DOWN)).then_inc(setup, 1)
            pool.wait_ge(setup, 4)

            def sum_over_all(n):
                pool.wait_ge(sum_done, n + 1)
                nc.gpsimd.partition_all_reduce(total[:, n:n + 1], part[:, n:n + 1], P, RADD).then_inc(sum_all, 1)

            def below(n, c):
                part_ = slice(c * E, (c + 1) * E)
                pool.wait_ge(theta_done, 2 * n + 2)
                if n == 2:
                    pool.wait_ge(gate_t, C)
                nc.gpsimd.tensor_scalar(flat[n][:, part_], raws[n][:, part_], ntheta[:, n:n + 1], None,
                                        ALU.is_lt).then_inc(neg_done, 1)

            sum_over_all(0)
            for t in range(T):
                k_lo(pool, 0, t)
            q_lo(pool, 0, 0)
            below(0, 2)
            q_lo(pool, 0, 1)
            below(0, 3)
            sum_over_all(1)
            below(1, 0)
            q_lo(pool, 0, 2)
            below(1, 1)
            pool.wait_ge(absmax_done, 4)
            nc.gpsimd.partition_all_reduce(wmax_all[:, 3:4], wmax[:, 3:4], P, RMAX).then_inc(absmax_all, 1)
            below(1, 2)
            q_lo(pool, 0, 3)
            below(1, 3)
            sum_over_all(2)
            below(2, 1)
            below(2, 3)
            all_pairs(pool, 0, pair_pool)
            last_head_pool(pool, 0)
            with pool.Fori(1, B) as b:
                layernorm_lo(pool, b)
                for t in range(T):
                    k_lo(pool, b, t)
                for t in range(T):
                    q_lo(pool, b, t)
                all_pairs(pool, b, pair_pool)
                last_head_pool(pool, b)

        def weight_parts():
            return [(w_raw[:, :, lo:lo + n], (w_qkv[:, 0, :, lo:lo + n], w_qkv[:, 1, :, lo:lo + n]))
                    for lo, n in ((0, 512), (512, 256), (768, 256))] + [
                        (wo_raw, (w_o[:, 0], w_o[:, 1]))]

        def front_act(act, b, sums_too=None):
            first = isinstance(b, int)

            def hi_part(t):
                act.wait_ge(xs_ready, b * T + t + 1)
                if t >= 2:
                    act.wait_ge(xT_ready, b * T + t - 1)
                elif t == 0:
                    ge(act, pv_done, b * H)
                nc.scalar.copy(x_tok[:, t % 2, 0, :], xs32[:, t % 2, :]).then_inc(xh_ready, 1)

            def xn_out(t):
                act.wait_ge(xT_ready, b * T + t + 1)
                nc.scalar.copy(xn_t[:, :, :, t * P:(t + 1) * P].rearrange("p s c n -> p (s c) n"),
                               bank16(5 - t % 2).rearrange("p (k n) -> p k n", n=P)).then_inc(xnT_ready, 1)

            hi_part(0)
            hi_part(1)
            xn_out(0)
            hi_part(2)
            xn_out(1)
            hi_part(3)
            xn_out(2)
            xn_out(3)
            if sums_too:
                sums_too(0, 0)
                sums_too(0, 1)
            for t in range(T):
                act.wait_ge(kr_ready, b * T + t + 1)
                ge(act, kT_ready, b * T + t - 1)
                stack = tk[t % 2]
                nc.scalar.copy(stack[:, H:HA, HD:2 * HD], r32[:, H:HA, :])
                nc.scalar.copy(stack[:, H:HA, 2 * HD:3 * HD], r32[:, H:HA, :]).then_inc(khi_done, 1)
                if t > 0:
                    k_out(act, b, t - 1)
            for t in range(T):
                act.wait_ge(qr_ready, b * T + t + 1)
                ge(act, qT_ready, (b * T + t - 1) * 2)
                stack = tk[t % 2]
                nc.scalar.copy(stack[:, 0:H, HD:2 * HD], r32[:, 0:H, :])
                nc.scalar.copy(stack[:, 0:H, 0:HD], r32[:, 0:H, :]).then_inc(qhi_done, 1)
                if t == 0:
                    k_out(act, b, T - 1)
                if sums_too and t < 2:
                    sums_too(1, 2 * t)
                    sums_too(1, 2 * t + 1)
                for g in range(2):
                    n = (b * T + t) * 2 + g
                    act.wait_ge(qT_ready, n + 1)
                    nc.scalar.copy(stk[0:STK, 8 * g:8 * g + 8, t * P:(t + 1) * P],
                                   bank16(4)[0:STK, :].rearrange("p (h n) -> p h n", n=P)
                                   ).then_inc(qstack_done, 1)

        def k_out(act, b, t):
            act.wait_ge(kT_ready, b * T + t + 1)
            nc.scalar.copy(stk[0:STK, H:HA, t * P:(t + 1) * P],
                           bank16(4)[0:STK, :].rearrange("p (h n) -> p h n", n=P)).then_inc(kstack_done, 1)

        def maxima_act(act, b):
            act.wait_ge(mT_ready, b + 1)
            ge(act, m_rows, b * 32)
            nc.scalar.copy(m_row[:], bank16(0)[0:2 * H, 0:S]).then_inc(m_row_s, 1)

        def head_act(act, n, j, early):
            def tanh_up():
                act.wait_ge(up_ready, n + 1)
                ge(act, t1_done, n - 1)
                nc.scalar.activation(th[:, j, :], psum[:, BU, :], ACT.Tanh, scale=TANH).then_inc(tanh_done, 1)

            if early:
                tanh_up()
            for half in range(2):
                act.wait_ge(sc_ready, 2 * n + half + 1)
                scores = psum[:, 2 * half:2 * half + 2, :]
                ge(act, pl_ready, 2 * n + half - 1)
                nc.scalar.activation(p32[:, half, :], scores, ACT.Exp, scale=SC).then_inc(p32_ready, 1)
                if half == 0:
                    ge(act, pv_done, n - 1)
                nc.scalar.activation(ph[:, j, 2 * half:2 * half + 2, :], scores, ACT.Exp,
                                     scale=SC).then_inc(exp_done, 1)
                if half == 0 and not early:
                    tanh_up()

        def pair_act(b, i):
            act = nc.scalar
            n = (b * (H // 2) + i) * 2
            if isinstance(i, int) and isinstance(b, int):
                act.wait_ge(coef_done, 1)
            head_act(act, n, 0, isinstance(i, int))
            head_act(act, n + 1, 1, False)

        @block.scalar
        def _(act):
            def hi_weights(n):
                src, dst = weight_parts()[n]
                nc.scalar.activation(dst[0], src, ACT.Copy, scale=winv[:, n:n + 1]).then_inc(whi_done, 1)

            def absolute_sums(n, c):
                nonlocal taken
                act.wait_ge(arrived[n][c], 16)
                for k in (2 * c, 2 * c + 1):
                    ge(act, sum_part, taken)
                    taken += 1
                    nc.scalar.activation(psum[:, 6:8, :], raws[n][:, k * E // 2:(k + 1) * E // 2], ACT.Abs,
                                         accum_out=sums[:, n, k:k + 1]).then_inc(sum_part, 1)

            taken = 0
            act.wait_ge(winv_done, 1)
            for n in range(3):
                hi_weights(n)
            front_act(act, 0, absolute_sums)
            act.wait_ge(winv_done, 2)
            hi_weights(3)
            for c in range(C):
                absolute_sums(2, c)
            maxima_act(act, 0)
            all_pairs(act, 0, pair_act)
            with act.Fori(1, B) as b:
                front_act(act, b)
                maxima_act(act, b)
                all_pairs(act, b, pair_act)

        def layernorm_stats(dve, b):
            dve.wait_ge(x_in_s, 16 * (b + 1))
            for t in range(T):
                nc.vector.bn_stats(stats[:, t, :], x_in[:, t, :]).then_inc(mv_done, 1)
            dve.wait_ge(mv_done, b * (2 * T) + T)
            nc.vector.memset(spare[:], 0.0)
            for t in range(T):
                nc.vector.bn_aggr(mv[:, t, :], stats[:, t, :]).then_inc(mv_done, 1)
            dve.wait_ge(mv_done, (b + 1) * (2 * T))
            nc.vector.tensor_scalar(rstd[:, 0, :], mv[:, :, 1], EPS, None, ALU.add).then_inc(eps_done, 1)

        def layernorm_scale(dve, b):
            dve.wait_ge(pow_done, b + 1)
            v, r, a, c, f = (rstd[:, k, :] for k in range(5))
            nc.vector.tensor_tensor(a, r, r, ALU.mult).then_inc(newton, 1)
            dve.wait_ge(newton, 3 * b + 1)
            nc.vector.tensor_tensor(c, a, v, ALU.mult).then_inc(newton, 1)
            dve.wait_ge(newton, 3 * b + 2)
            nc.vector.tensor_scalar(f, c, -0.5 * 2.0 ** X_UP, 1.5 * 2.0 ** X_UP, ALU.mult,
                                    ALU.add).then_inc(newton, 1)
            dve.wait_ge(newton, 3 * b + 3)
            nc.vector.tensor_tensor(rstd[:, 5, :], f, r, ALU.mult).then_inc(rstd_done, 1)

        def layernorm_apply(dve, b, t):
            if t == 0:
                dve.wait_ge(rstd_done, b + 1)
                ge(dve, pv_done, b * H - 1)
            if t >= 2:
                dve.wait_ge(xl_ready, b * T + t - 1)
            nc.vector.tensor_scalar(xs32[:, t % 2, :], x_in[:, t, :], mv[:, t, 0:1], rstd[:, 5, t:t + 1],
                                    ALU.subtract, ALU.mult).then_inc(xs_ready, 1)

        def rope(dve, b, t, src, h0, h1, turned_, step, ready, lo_done):
            n = b * T + t
            ge(dve, ready, n)
            for dst, tab in ((rope_a, cos_t), (rope_b, sin_t)):
                nc.vector.tensor_tensor(dst[:, h0:h1, :], src, tab[:, t:t + 1, :].to_broadcast([P, h1 - h0, HD]),
                                        ALU.mult).then_inc(step, 1)
            turned_()
            dve.wait_ge(step, 2 * (n + 1))
            ge(dve, lo_done, n)
            even, odd = slice(0, HD, 2), slice(1, HD, 2)
            nc.vector.tensor_tensor(r32[:, h0:h1, even], rope_a[:, h0:h1, even], rope_b[:, h0:h1, odd], ALU.add)
            nc.vector.tensor_tensor(r32[:, h0:h1, odd], rope_a[:, h0:h1, odd], rope_b[:, h0:h1, even],
                                    ALU.add).then_inc(ready, 1)

        def kv_dve(dve, b, t):
            n = b * T + t
            if isinstance(b, int) and t == 0:
                dve.wait_ge(const_in, 48)
            dve.wait_ge(kv_ready, n + 1)
            k = psum[:, t, 0:KV * HD].rearrange("p (h d) -> p h d", d=HD)
            v = psum[:, t, KV * HD:].rearrange("p (h d) -> p h d", d=HD)
            if t == 0 and not isinstance(b, int):
                dve.wait_ge(pl_ready, b * 2 * H)

            def v_parts():
                vh, vl = v_all[:, t, :, 0:HD], v_all[:, t, :, HD:2 * HD]
                down = 2.0 ** -(X_UP + W_UP)
                nc.vector.tensor_scalar(vh, v, down, None, ALU.mult).then_inc(vh_done, 1)
                dve.wait_ge(vh_done, n + 1)
                nc.vector.scalar_tensor_tensor(vl, v, down, vh, ALU.mult, ALU.subtract).then_inc(kv_used, 1)

            rope(dve, b, t, k, H, HA, v_parts, k_step, kr_ready, klo_done)

        def q_dve(dve, b, t):
            dve.wait_ge(q_ready, b * T + t + 1)
            rope(dve, b, t, psum[:, 5, :].rearrange("p (h d) -> p h d", d=HD), 0, H, lambda: None,
                 q_step, qr_ready, qlo_done)

        def attn_t_dve(dve, b, t):
            dve.wait_ge(aT_ready, (b - 1) * T + t + 1)
            if t == 0:
                dve.wait_ge(hid_done, b * 2 * H)
            nc.vector.tensor_copy(a_t[:, :, :, t * P:(t + 1) * P].rearrange("p s c n -> p (s c) n"),
                                  bank16(t).rearrange("p (k n) -> p k n", n=P)).then_inc(attnT_ready, 1)

        Q_ROPE = 1

        def maxima_dve(dve, b, between):
            for g in range(MAX_GROUPS):
                t, h = g // KV, g % KV * 2
                dve.wait_ge(mx_ready, b * MAX_GROUPS + g + 1)
                nc.vector.tensor_reduce(mx[:, t, h:h + 2], psum[:, 2 * (g % 2):2 * (g % 2) + 2, :], AX.X,
                                        ALU.max).then_inc(mx_done, 1)
                if g % KV == Q_ROPE and t + 1 < T:
                    q_dve(dve, b, t + 1)
                for f in between.get(g, ()):
                    f()
            down = 2.0 ** -MAX_DOWN
            dve.wait_ge(mx_done, (b + 1) * MAX_GROUPS)
            nc.vector.tensor_scalar(m_tok[:, :, 0, :], mx[:], down, None, ALU.mult).then_inc(mh_done, 1)
            dve.wait_ge(mh_done, b + 1)
            nc.vector.scalar_tensor_tensor(m_tok[:, :, 1, :], mx[:], down, m_tok[:, :, 0, :], ALU.mult,
                                           ALU.subtract).then_inc(ml_done, 1)
            for f in between.get(MAX_GROUPS, ()):
                f()

        def y_after(dve, b):
            return {0: [lambda: y_down(dve, b, 1)], 10: [lambda: y_down(dve, b, 2)],
                    20: [lambda: y_down(dve, b, 3)], 23: [lambda: y_attn(dve, b, 0)],
                    26: [lambda: y_attn(dve, b, 1)], 29: [lambda: y_attn(dve, b, 2)],
                    MAX_GROUPS: [lambda: y_attn(dve, b, 3)]}

        def y_down(dve, b, t):
            n = (b - 1) * T + t
            dve.wait_ge(down_ready, n + 1)
            nc.vector.scalar_tensor_tensor(y[:, t, :], psum[:, DOWN_BANK[t], :], CD, y[:, t, :], ALU.mult,
                                           ALU.add).then_inc(y1_done, 1)

        def y_attn(dve, b, t):
            n = (b - 1) * T + t
            dve.wait_ge(wo_ready, n + 1)
            dve.wait_ge(y1_done, n + 1)
            nc.vector.scalar_tensor_tensor(y[:, t, :], psum[:, WO_BANK[t], :], CA, y[:, t, :], ALU.mult,
                                           ALU.add).then_inc(y_ready, 1)

        def normalise(dve, n, j):
            dve.wait_ge(pv_done, n + 1)
            o = psum[:, 6 + j, 0:T * (2 * HD + 1)].rearrange("p (t d) -> p t d", t=T)
            ge(dve, ef_done, n)
            nc.vector.reciprocal(rden[:], o[:, :, 2 * HD:2 * HD + 1]).then_inc(rden_done, 1)
            dve.wait_ge(rden_done, n + 1)
            ge(dve, attn_done, 2 * (n - 1))
            r = rden[:].to_broadcast([P, T, HD])
            nc.vector.tensor_tensor(norm_e[:, j], o[:, :, 0:HD], r, ALU.mult).then_inc(e_done, 1)
            dve.wait_ge(e_done, n + 1)
            nc.vector.tensor_tensor(norm_f[:, j], o[:, :, HD:2 * HD], r, ALU.mult).then_inc(ef_done, 1)

        def head_dve(dve, n, j, first, early=False):
            def lo_part(half):
                dve.wait_ge(exp_done, 2 * n + half + 1)
                if half == 0:
                    ge(dve, pv_done, n - 1)
                nc.vector.tensor_tensor(pl[:, j, 2 * half:2 * half + 2, :].rearrange("p a b -> p (a b)"),
                                        p32[:, half, :],
                                        ph[:, j, 2 * half:2 * half + 2, :].rearrange("p a b -> p (a b)"),
                                        ALU.subtract).then_inc(pl_ready, 1)

            if not early:
                lo_part(0)
            dve.wait_ge(tanh_done, n + 1)
            ge(dve, h32_ready, n)
            nc.vector.scalar_tensor_tensor(t1, th[:, j, :], 1.0, psum[:, BU, :], ALU.add,
                                           ALU.mult).then_inc(t1_done, 1)
            dve.wait_ge(t1_done, n + 1)
            dve.wait_ge(gate_ready, n + 1)
            ge(dve, hid_done, 2 * (n - 1))
            nc.vector.scalar_tensor_tensor(h32[:, j, :], t1, 2.0 ** -(H_DOWN + 2 * X_UP), psum[:, BG, :],
                                           ALU.mult, ALU.mult).then_inc(h32_ready, 1)
            if early:
                lo_part(0)
            lo_part(1)
            if not first:
                normalise(dve, n - 1, 1 - j)

        last_ternary = []

        def pair_dve(b, i):
            dve = nc.vector
            n = (b * (H // 2) + i) * 2
            head_dve(dve, n, 0, isinstance(i, int), isinstance(i, int))
            if isinstance(i, int):
                if isinstance(b, int):
                    for f in last_ternary:
                        f()
                layernorm_stats(dve, b + 1)
            head_dve(dve, n + 1, 1, False)
            if isinstance(i, int):
                layernorm_scale(dve, b + 1)

        def last_head_dve(dve, b):
            normalise(dve, b * H + H - 1, 1)

        @block.vector
        def _(dve):
            def largest(n, s_in):
                dve.wait_ge(s_in, 16)
                nc.vector.tensor_reduce(wmax[:, n:n + 1], weight_parts()[n][0], AX.XY, ALU.max,
                                        apply_absolute_value=True).then_inc(absmax_done, 1)

            def exponents(lo, hi, k):
                some = slice(lo, hi)
                dve.wait_ge(absmax_all, k + 1)
                nc.vector.tensor_scalar(wmax_all[:, some], wmax_all[:, some], 2.0 ** -100, 2.0 ** 100,
                                        ALU.max, ALU.min).then_inc(winv_step, 1)
                dve.wait_ge(winv_step, 3 * k + 1)
                nc.vector.tensor_scalar(wpow[:, some].bitcast(U32), wmax_all[:, some].bitcast(U32),
                                        0x7F800000, None, ALU.bitwise_and).then_inc(winv_step, 1)
                dve.wait_ge(winv_step, 3 * k + 2)
                nc.vector.reciprocal(winv[:, some], wpow[:, some]).then_inc(winv_step, 1)
                dve.wait_ge(winv_step, 3 * k + 3)
                nc.vector.tensor_scalar(winv[:, some], winv[:, some], 2.0 ** W_UP, None,
                                        ALU.mult).then_inc(winv_done, 1)
                dve.wait_ge(winv_done, k + 1)

            def lo_weights(n):
                src, dst = weight_parts()[n]
                dve.wait_ge(whi_done, n + 1)
                nc.vector.scalar_tensor_tensor(dst[1], src, winv[:, n:n + 1], dst[0], ALU.mult,
                                               ALU.subtract).then_inc(wlo_done, 1)

            def more_sums(n, c):
                dve.wait_ge(arrived[n][c], 16)
                nc.vector.tensor_reduce(sums[:, n, 2 * c:2 * c + 2],
                                        raws[n][:, c * E:(c + 1) * E].rearrange("p (g k) -> p g k", g=2), AX.X, ALU.add,
                                        apply_absolute_value=True).then_inc(more_sum, 1)

            def thresholds(n, by_act, by_dve):
                dve.wait_ge(sum_part, by_act)
                ge(dve, more_sum, by_dve)
                nc.vector.tensor_reduce(part[:, n:n + 1], sums[:, n, :], AX.X, ALU.add).then_inc(sum_done, 1)
                dve.wait_ge(sum_all, n + 1)
                nc.vector.tensor_scalar(scale[:, n:n + 1], total[:, n:n + 1], 1.0 / (E * D), 1e-8, ALU.mult,
                                        ALU.add).then_inc(theta_done, 1)
                dve.wait_ge(theta_done, 2 * n + 1)
                nc.vector.tensor_scalar(theta[:, n:n + 1], scale[:, n:n + 1], 0.5, None, ALU.mult)
                nc.vector.tensor_scalar(ntheta[:, n:n + 1], scale[:, n:n + 1], -0.5, None,
                                        ALU.mult).then_inc(theta_done, 1)
                dve.wait_ge(theta_done, 2 * n + 2)

            def ternary(n, c):
                nonlocal own
                part_ = slice(c * E, (c + 1) * E)
                if (n, c) in BELOW_BY_DVE:
                    if n == 2:
                        dve.wait_ge(gate_t, C)
                    nc.vector.tensor_scalar(flat[n][:, part_], raws[n][:, part_], ntheta[:, n:n + 1], None,
                                            ALU.is_lt).then_inc(own_neg, 1)
                    own += 1
                    dve.wait_ge(own_neg, own)
                else:
                    dve.wait_ge(neg_done, BELOW_BY_POOL.index((n, c)) + 1)
                nc.vector.scalar_tensor_tensor(flat[n][:, part_], raws[n][:, part_], theta[:, n:n + 1],
                                               flat[n][:, part_], ALU.is_gt,
                                               ALU.subtract).then_inc(turned[n], 1)

            def coefficients():
                def step(out_, a, b_):
                    nonlocal k
                    nc.vector.tensor_tensor(out_, a, b_, ALU.mult).then_inc(coef_step, 1)
                    k += 1
                    dve.wait_ge(coef_step, k)
                k = 0
                step(coef[:, 4:5], wpow[:, WQ:WQ + 1], wpow[:, WK:WK + 1])
                step(coef[:, 5:6], wpow[:, WV:WV + 1], wpow[:, WO:WO + 1])
                step(coef[:, 6:7], scale[:, 0:1], scale[:, 1:2])
                step(coef[:, 7:8], coef[:, 6:7], scale[:, 2:3])
                nc.vector.tensor_scalar(SC, coef[:, 4:5], float(HD) ** -0.5, None, ALU.mult)
                nc.vector.tensor_scalar(TANH, scale[:, 0:1], 0.5 * 2.0 ** -X_UP, None, ALU.mult)
                nc.vector.tensor_scalar(CD, coef[:, 7:8], 2.0 ** (H_DOWN - 1), None, ALU.mult)
                nc.vector.tensor_scalar(CA, coef[:, 5:6], 2.0 ** -W_UP, None, ALU.mult).then_inc(coef_done, 1)

            own = 0
            layernorm_stats(dve, 0)
            for n, s_in in enumerate((wq_in, wk_in, wv_in)):
                largest(n, s_in)
            exponents(0, 3, 0)
            layernorm_scale(dve, 0)
            layernorm_apply(dve, 0, 0)
            layernorm_apply(dve, 0, 1)
            for n in range(3):
                lo_weights(n)
            layernorm_apply(dve, 0, 2)
            layernorm_apply(dve, 0, 3)
            more_sums(0, 2)
            more_sums(0, 3)
            kv_dve(dve, 0, 0)
            thresholds(0, 4, 2)
            for t in range(1, T):
                kv_dve(dve, 0, t)
            q_dve(dve, 0, 0)
            ternary(0, 0)
            ternary(0, 1)
            maxima_dve(dve, 0, {
                1: [lambda: ternary(0, 2)],
                4: [lambda: ternary(0, 3)],
                5: [lambda: thresholds(1, 4 + 2 * C, 2)],
                7: [lambda: largest(3, wo_in)],
                9: [lambda: ternary(1, 0)],
                12: [lambda: ternary(1, 1)],
                15: [lambda: exponents(3, 4, 1)],
                17: [lambda: ternary(1, 2)],
                21: [lambda: lo_weights(3)],
                22: [lambda: ternary(1, 3)],
                26: [lambda: thresholds(2, 4 + 4 * C, 2), coefficients],
                28: [lambda: ternary(2, 0)],
                MAX_GROUPS: [lambda: ternary(2, 2)]})
            last_ternary.extend((lambda: ternary(2, 1), lambda: ternary(2, 3)))
            all_pairs(dve, 0, pair_dve)
            with dve.Fori(1, B) as b:
                layernorm_apply(dve, b, 0)
                layernorm_apply(dve, b, 1)
                last_head_dve(dve, b - 1)
                dve.wait_ge(y_in, 16 * b)
                y_down(dve, b, 0)
                layernorm_apply(dve, b, 2)
                layernorm_apply(dve, b, 3)
                for t in range(T):
                    kv_dve(dve, b, t)
                q_dve(dve, b, 0)
                for t in range(T):
                    attn_t_dve(dve, b, t)
                maxima_dve(dve, b, y_after(dve, b))
                all_pairs(dve, b, pair_dve)
            last_head_dve(dve, B - 1)
            dve.wait_ge(y_in, 16 * B)
            y_down(dve, B, 0)
            for t in range(T):
                attn_t_dve(dve, B, t)
            for t in range(1, T):
                y_down(dve, B, t)
            for t in range(T):
                y_attn(dve, B, t)

        def pe_front(pe, b):
            first = isinstance(b, int)

            def transpose8(bank, src, inc):
                for k in range(8):
                    m = nc.tensor.transpose(bank16(bank)[:, k * P:(k + 1) * P], src(k), ident[:])
                m.then_inc(inc, 1)

            def x_t(t):
                pe.wait_ge(xl_ready, b * T + t + 1)
                if t >= 2:
                    pe.wait_ge(xnT_ready, b * T + t - 1)
                elif t == 0:
                    ge(pe, h32_ready, b * H)
                elif not first:
                    pe.wait_ge(y1_done, (b - 1) * T + 1)
                transpose8(5 - t % 2, lambda k: x_tok[:, t % 2, k // C, (k % C) * P:(k % C + 1) * P],
                           xT_ready)

            def kv(t):
                pe.wait_ge(xnT_ready, b * T + t + 1)
                if t == 0:
                    ge(pe, exp_done, b * 2 * H)
                projection(t, t, slice(512, 1024), kv_ready, range(3 * C))

            def projection(t, bank, cols, done, steps):
                for k in steps:
                    c, (xp, wp) = k // 3, ((0, 0), (0, 1), (1, 0))[k % 3]
                    m = nc.tensor.matmul(psum[:, bank, :], xn_t[:, xp, c, t * P:(t + 1) * P],
                                         w_qkv[:, wp, c, cols], start=k == 0, stop=k == 3 * C - 1)
                    if k == 3 * C - 1:
                        m.then_inc(done, 1)

            def q(t, steps=range(3 * C)):
                if 0 in steps and t == 0:
                    pe.wait_ge(xnT_ready, (b + 1) * T)
                elif 0 in steps:
                    pe.wait_ge(q_step, 2 * (b * T + t))
                projection(t, 5, slice(0, 512), q_ready, steps)

            def stack_t(src, done):
                for h in range(8):
                    m = nc.tensor.transpose(bank16(4)[0:STK, h * P:(h + 1) * P], src[:, h, :], ident[:])
                m.then_inc(done, 1)

            def k_t(t):
                pe.wait_ge(klo_done, b * T + t + 1)
                if t == 0:
                    pe.wait_ge(xnT_ready, (b + 1) * T)
                else:
                    pe.wait_ge(kstack_done, b * T + t)
                stack_t(tk[t % 2][:, H:HA, :], kT_ready)

            def q_t(t, g):
                pe.wait_ge(qlo_done, b * T + t + 1)
                if t == 0 and g == 0:
                    pe.wait_ge(kstack_done, (b + 1) * T)
                else:
                    pe.wait_ge(qstack_done, (b * T + t) * 2 + g)
                stack_t(tk[t % 2][:, 8 * g:8 * g + 8, :], qT_ready)

            def maxima(g):
                t, i = g // KV, g % KV
                if i == 0:
                    pe.wait_ge(qstack_done, (b * T + t + 1) * 2)
                if g == 0:
                    pe.wait_ge(kstack_done, (b + 1) * T)
                    pe.wait_ge(kv_used, (b + 1) * T)
                    ge(pe, attnT_ready, b * T)
                if g >= 2:
                    pe.wait_ge(mx_done, b * MAX_GROUPS + g - 1)
                for u in range(2):
                    m = nc.tensor.matmul(psum[:, 2 * (g % 2) + u, :],
                                         stk[0:STK, 2 * i + u, t * P:(t + 1) * P],
                                         stk[0:STK, H + i, :], start=True, stop=True)
                m.then_inc(mx_ready, 1)

            if first:
                tail = []
            else:
                tail = [f for t in (1, 2, 3) for f in down_steps(pe, b, t)]
                tail += [f for t in range(T) for f in wo_steps(pe, b, t)]

            def some(n):
                run_tail(pe, tail[:n])
                del tail[:n]

            if first:
                pe.wait_ge(const_in, 48)
                for t in range(T):
                    x_t(t)
                pe.wait_ge(wlo_done, 3)
            else:
                run_tail(pe, down_steps(pe, b, 0)[PE_EARLY:])
                x_t(0)
                some(4)
                x_t(1)
                kv(0)
                x_t(2)
                kv(1)
                x_t(3)
            if first:
                kv(0)
                kv(1)
            kv(2)
            k_t(0)
            kv(3)
            k_t(1)
            q(0)
            k_t(2)
            k_t(3)
            if not first:
                for t in range(T):
                    attn_t_pe(pe, b, t)
            some(28)
            q_t(0, 0)
            some(8)
            q_t(0, 1)
            q(1)
            for g in range(MAX_GROUPS):
                maxima(g)
                t, i = g // KV, g % KV
                if i >= KV // 2 and t + 2 < T:
                    q(t + 2, range((i - KV // 2) * 3, (i - KV // 2) * 3 + 3))
                    some(FILL_Q[i - KV // 2])
                else:
                    some(FILL)
                if i in (Q_TRANSPOSE, Q_TRANSPOSE + 1) and t + 1 < T:
                    q_t(t + 1, i - Q_TRANSPOSE)
            some(len(tail))
            if first:
                pe.wait_ge(up_t, C)
            up_pe(pe, b * H, 0)
            pe.wait_ge(ml_done, b + 1)
            for t in range(T):
                m = nc.tensor.transpose(bank16(0)[0:2 * H, t * P:(t + 1) * P],
                                        m_tok[:, t, :, :].rearrange("p s h -> p (s h)"), ident[:])
            m.then_inc(mT_ready, 1)

        def run_tail(pe, steps):
            for step in steps:
                step()

        def attn_t_pe(pe, b, t):
            if t == 0:
                pe.wait_ge(attn_done, b * 2 * H)
                pe.wait_ge(exp_done, b * 2 * H)
            if not isinstance(b, int):
                pe.wait_ge(kv_used, b * T + t + 1)
            for k in range(8):
                m = nc.tensor.transpose(bank16(t)[:, k * P:(k + 1) * P],
                                        a_tok[:, k // C, t, (k % C) * P:(k % C + 1) * P], ident[:])
            m.then_inc(aT_ready, 1)

        def down_steps(pe, b, t):
            def step(k):
                def go():
                    e, s_ = k // 2, k % 2
                    if t == 0 and k == 0:
                        pe.wait_ge(t1_done, b * H)
                        pe.wait_ge(hid_done, b * 2 * H - 2)
                    if t == 0 and e == ET - 1 and s_ == 0:
                        pe.wait_ge(hid_done, b * 2 * H)
                    if t in (1, 2) and k == 0:
                        pe.wait_ge(ef_done, b * H)
                    if t == 3 and k == 0:
                        pe.wait_ge(y1_done, (b - 1) * T + 2)
                    m = nc.tensor.matmul(psum[:, DOWN_BANK[t], :], hid[:, s_, e, t * P:(t + 1) * P],
                                         t_down[:, e, :], start=k == 0, stop=k == 2 * ET - 1)
                    if k == 2 * ET - 1:
                        m.then_inc(down_ready, 1)
                return go
            return [step(k) for k in range(2 * ET)]

        def wo_steps(pe, b, t):
            def step(k):
                def go():
                    c, (ap, wp) = k // 3, ((0, 0), (0, 1), (1, 0))[k % 3]
                    if k == 0 and t == 0:
                        pe.wait_ge(attnT_ready, b * T)
                    if k == 0 and t < 2:
                        pe.wait_ge(y1_done, (b - 1) * T + t + 3)
                    if k == 0 and t >= 2:
                        pe.wait_ge(y_ready, (b - 1) * T + t - 1)
                    m = nc.tensor.matmul(psum[:, WO_BANK[t], :], a_t[:, ap, c, t * P:(t + 1) * P],
                                         w_o[:, wp, c, :], start=k == 0, stop=k == 3 * C - 1)
                    if k == 3 * C - 1:
                        m.then_inc(wo_ready, 1)
                return go
            return [step(k) for k in range(3 * C)]

        def pe_pv(pe, n, j, g):
            pe.wait_ge(pl_ready, 2 * n + 2)
            ge(pe, ef_done, n - 1)
            for t in range(T):
                for kt in range(T):
                    for s_, p_part in enumerate((ph, pl)):
                        m = nc.tensor.matmul(psum[:, 6 + j, t * (2 * HD + 1):(t + 1) * (2 * HD + 1)],
                                             p_part[:, j, kt, t * P:(t + 1) * P], v_all[:, kt, g, :],
                                             start=kt == 0 and s_ == 0, stop=kt == T - 1 and s_ == 1)
            m.then_inc(pv_done, 1)

        FILL, FILL_Q = 4, (1, 1, 1, 1)
        Q_TRANSPOSE = 5
        PE_EARLY = 8

        def pe_last(pe, b):
            run_tail(pe, down_steps(pe, b, 0)[:PE_EARLY])
            pe_pv(pe, b * H - 1, 1, KV - 1)

        def scores_pe(pe, b, n, h, i, first):
            for half in range(2):
                if not first:
                    pe.wait_ge(exp_done, 2 * (n - 1) + half + 1)
                elif half == 0:
                    pe.wait_ge(m_row_s, b + 1)
                    pe.wait_ge(m_rows, 32 * (b + 1))
                for u in range(2):
                    kt = 2 * half + u
                    m = nc.tensor.matmul(psum[:, kt, :], stk[0:ROWS, H + i, kt * P:(kt + 1) * P],
                                         stk[0:ROWS, h, :], start=True, stop=True)
                m.then_inc(sc_ready, 1)

        def up_gate_pe(pe, n, h):
            up_pe(pe, n, h)
            gate_pe(pe, n, h)

        def up_pe(pe, n, h):
            ge(pe, t1_done, n)
            ternary_product(t_up, BU, h, up_ready)

        def gate_pe(pe, n, h):
            ge(pe, h32_ready, n)
            ternary_product(t_gate, BG, h, gate_ready)

        def ternary_product(w, bank, h, done):
            for c in range(C):
                for s_ in range(2):
                    m = nc.tensor.matmul(psum[:, bank, :], w[:, c, bass.ts(h, P)], xn_t[:, s_, c, :],
                                         start=c == 0 and s_ == 0, stop=c == C - 1 and s_ == 1)
            m.then_inc(done, 1)

        def pair_pe(b, i):
            pe = nc.tensor
            n = (b * (H // 2) + i) * 2
            start = isinstance(i, int)
            if start:
                if isinstance(b, int):
                    pe.wait_ge(gate_t, C)
                    pe.wait_ge(setup, 4)
                gate_pe(pe, n, i * 2)
                up_pe(pe, n + 1, i * 2 + 1)
                scores_pe(pe, b, n, i * 2, i, True)
                gate_pe(pe, n + 1, i * 2 + 1)
                scores_pe(pe, b, n + 1, i * 2 + 1, i, False)
            else:
                scores_pe(pe, b, n, i * 2, i, False)
                up_gate_pe(pe, n, i * 2)
                pe_pv(pe, n - 1, 1, i - 1)
                scores_pe(pe, b, n + 1, i * 2 + 1, i, False)
                up_gate_pe(pe, n + 1, i * 2 + 1)
            if start:
                ge(pe, y_ready, b * T)
            pe_pv(pe, n, 0, i)

        @block.tensor
        def _(pe):
            pe_front(pe, 0)
            all_pairs(pe, 0, pair_pe)
            pe.wait_ge(down_t, C)
            pe_last(pe, 1)
            with pe.Fori(1, B) as b:
                pe_front(pe, b)
                all_pairs(pe, b, pair_pe)
                pe_last(pe, b + 1)
            run_tail(pe, down_steps(pe, B, 0)[PE_EARLY:])
            run_tail(pe, down_steps(pe, B, 1))
            for t in range(T):
                attn_t_pe(pe, B, t)
            for t in (2, 3):
                run_tail(pe, down_steps(pe, B, t))
            for t in range(T):
                run_tail(pe, wo_steps(pe, B, t))


def rope_tables():
    inv_freq = (1.0 / np.float32(10000.0) ** (np.arange(0, HD, 2, dtype=np.float32) / np.float32(HD))).astype(np.float32)
    angle = (np.arange(S, dtype=np.float32)[:, None] * inv_freq[None, :]).astype(np.float32)
    down = np.float32(2.0 ** -(X_UP + W_UP))
    cos, sin = np.cos(angle) * down, np.sin(angle) * down
    c = np.repeat(cos, 2, axis=1).astype(np.float32)
    sn = np.stack([sin, -sin], axis=2).reshape(S, HD).astype(np.float32)
    return c, sn


def kernel(L0_attn_x, L0_attn_wq, L0_attn_wk, L0_attn_wv, L0_attn_wo, L0_ffn_W_up, L0_ffn_W_gate, L0_ffn_W_down):
    import concourse.bacc as bacc
    from concourse.bass_utils import run_bass_kernel_spmd

    c, sn = rope_tables()
    arrays = {
        "x": L0_attn_x, "wq": L0_attn_wq, "wk": L0_attn_wk, "wv": L0_attn_wv, "wo": L0_attn_wo,
        "w_up_t": np.asarray(L0_ffn_W_up).T, "w_gate_t": np.asarray(L0_ffn_W_gate).T,
        "w_down_t": np.asarray(L0_ffn_W_down).T,
        "rope_c": c, "rope_s": sn, "ident": np.eye(P, dtype=np.float16),
    }
    arrays = {k: np.ascontiguousarray(v) for k, v in arrays.items()}
    nc = bacc.Bacc("TRN2", target_bir_lowering=False, num_devices=1)
    aps = [nc.dram_tensor(k, v.shape, mybir.dt.from_np(v.dtype), kind="ExternalInput").ap()
           for k, v in arrays.items()]
    out = nc.dram_tensor("out", (B, S, D), F32, kind="ExternalOutput").ap()
    build(nc, *aps, out)
    r = run_bass_kernel_spmd(nc, [arrays], core_ids=[0])
    return r.results[0]["out"]
```

```python
import concourse.bass as bass
from concourse import mybir
from contextlib import ExitStack
import numpy as np

F32 = mybir.dt.float32
F16 = mybir.dt.float16
U32 = mybir.dt.uint32
ALU = mybir.AluOpType
ACT = mybir.ActivationFunctionType
AX = mybir.AxisListType
RMAX = bass.bass_isa.ReduceOp.max
RADD = bass.bass_isa.ReduceOp.add

P = 128
B, S, D = 4, 512, 512
H, KV, HD = 16, 8, 32
HA = H + KV
E = 2048
C = D // P
T = S // P
ET = E // P
STK = 3 * HD
ROWS = STK + 2
EPS = 1e-5

X_UP = 11
W_UP = 14
MAX_DOWN = 9
H_DOWN = 4
MAX_GROUPS = T * KV


def build(nc, x, wq, wk, wv, wo, w_up_t, w_gate_t, w_down_t, rope_c, rope_s, ident_in, out):
    ctx = ExitStack()
    with ctx:
        def sb(name, shape, dt):
            return ctx.enter_context(nc.sbuf_tensor(name, shape, dt))

        def sem(name):
            return ctx.enter_context(nc.semaphore(name))

        def as16(ap):
            return ap.bitcast(F16)

        x_v = x.rearrange("b (t p) d -> b p t d", p=P)
        out_v = out.rearrange("b (t p) d -> b p t d", p=P)

        t_up = sb("t_up", [P, C, E], F16)
        t_gate = sb("t_gate", [P, C, E], F16)
        w_qkv = sb("w_qkv", [P, 2, C, 1024], F16)
        w_o = sb("w_o", [P, 2, C, D], F16)
        ident = sb("identity", [P, P], F16)
        cos_t = sb("cos_t", [P, T, HD], F32)
        sin_t = sb("sin_t", [P, T, HD], F32)
        v_all = sb("v_all", [P, T, KV, 2 * HD + 1], F16)
        xn_t = sb("xn_t", [P, 2, C, S], F16)
        x_in = sb("x_in", [P, T, D], F32)

        late = sb("late", [P, 8192], F32)
        t_down = as16(late[:, 0:4096]).rearrange("p (e d) -> p e d", e=ET)
        a_tok = as16(late[:, 4096:6144]).rearrange("p (s t d) -> p s t d", s=2, t=T)
        y = late[:, 6144:8192].rearrange("p (t d) -> p t d", t=T)

        hid_raw = sb("hid_raw", [P, 8192], F32)
        hid = as16(hid_raw[:, :]).rearrange("p (e s n) -> p e s n", s=2, e=ET)

        stk_raw = sb("stk_raw", [P, 6144], F32)
        stk = as16(stk_raw[:, :]).rearrange("p (h n) -> p h n", h=HA)
        w_raw = stk_raw[:, 0:4096].rearrange("p (c n) -> p c n", c=C)

        p32 = sb("p32", [P, 2, 2 * S], F32)
        ph = sb("ph", [P, 2, T, S], F16)
        pl = sb("pl", [P, 2, T, S], F16)
        rope_a = p32[:, 0, 0:HA * HD].rearrange("p (h d) -> p h d", d=HD)
        rope_b = p32[:, 1, 0:HA * HD].rearrange("p (h d) -> p h d", d=HD)
        xs32 = ph[:, 0, :, :].rearrange("p a b -> p (a b)").bitcast(F32).rearrange(
            "p (n d) -> p n d", n=2)
        x_tok = ph[:, 1, :, :].rearrange("p a (s d) -> p (a s) d", s=1).rearrange(
            "p (n s) d -> p n s d", n=2)
        pl_flat = pl[:, :, :, :].rearrange("p a b c -> p (a b c)")
        r32 = pl_flat[:, 0:2 * HA * HD].bitcast(F32).rearrange("p (h d) -> p h d", d=HD)
        tk = (pl_flat[:, 2 * HA * HD:2 * HA * HD + HA * STK].rearrange("p (h d) -> p h d", d=STK),
              ph[:, :, :, :].rearrange("p a b c -> p (a b c)")[:, 0:HA * STK].rearrange(
                  "p (h d) -> p h d", d=STK))

        act_raw = sb("act_raw", [P, 5, D], F32)
        th = act_raw[:, 0:2, :]
        t1 = act_raw[:, 2, :]
        h32 = act_raw[:, 3:5, :]
        a_t = act_raw[:, 0:4, :].rearrange("p a b -> p (a b)").bitcast(F16).rearrange(
            "p (s c n) -> p s c n", s=2, c=C)
        wo_raw = act_raw[:, 0:4, :]

        norm_e = sb("norm_e", [P, 2, T, HD], F32)
        norm_f = sb("norm_f", [P, 2, T, HD], F32)
        norm_a = sb("norm_a", [P, T, HD], F32)
        rden = sb("rden", [P, T, 1], F32)
        mx = sb("mx", [P, T, H], F32)
        m_tok = sb("m_tok", [P, T, 2, H], F16)
        m_row = sb("m_row", [2 * H, S], F16)
        stats = sb("stats", [P, T, 6], F32)
        mv = sb("mv", [P, T, 2], F32)
        rstd = sb("rstd", [P, 6, T], F32)
        sums = sb("sums", [P, 3, 2 * C], F32)
        part = sb("part", [P, 3], F32)
        total = sb("total", [P, 3], F32)
        scale = sb("scale", [P, 3], F32)
        theta = sb("theta", [P, 3], F32)
        ntheta = sb("ntheta", [P, 3], F32)
        wmax = sb("wmax", [P, 4], F32)
        wmax_all = sb("wmax_all", [P, 4], F32)
        wpow = sb("wpow", [P, 4], F32)
        winv = sb("winv", [P, 4], F32)
        coef = sb("coef", [P, 8], F32)
        one = sb("one", [P, 1], F32)
        spare = sb("spare", [P, 1], F32)
        minus_half = sb("minus_half", [P, T], F32)
        SC, TANH, CD, CA = (coef[:, n:n + 1] for n in (0, 1, 2, 3))
        WQ, WK, WV, WO = range(4)

        psum = ctx.enter_context(nc.psum_tensor("psum", [P, 8, 512], F32))
        BU, BG = 4, 5
        DOWN_BANK, WO_BANK = (4, 7, 6, 7), (6, 7, 6, 7)

        def bank16(n):
            return psum[:, n, :].bitcast(F16)

        BEFORE = (8, 14, 8)
        BESIDE = [4, 3, 6, 12, 0, 0, 0, 0,
                  4, 3, 4, 10, 0, 0, 0, 0,
                  4, 3, 4, 10, 4, 3, 4, 3,
                  4, 4, 4, 4, 4, 4, 4, 4]
        Y_LATE = 1
        Q_ROPE = 1
        Q_TRANSPOSE = 5
        PE_EARLY = 16

        names = """ident_in_s const_in wq_in wk_in wv_in wo_in x_in_s y_in y_out
            absmax_done absmax_all winv_done whi_done wlo_done
            sum_part sum_done sum_all theta_done neg_done up_t gate_t down_t coef_done setup
            mv_done eps_done pow_done newton rstd_done xs_ready xh_ready xl_ready xT_ready xnT_ready
            kv_ready k_step vh_done kv_used kr_ready khi_done klo_done kT_ready kstack_done
            q_ready q_step qr_ready qhi_done qlo_done qT_ready qstack_done
            mx_ready mx_done mh_done ml_done mT_ready m_row_s m_rows
            sc_ready exp_done pl_ready pv_done
            up_ready gate_ready tanh_done t1_done h32_ready hid_done
            rden_done e_done ef_done attn_done
            aT_ready attnT_ready down_ready wo_ready y1_done y_ready""".split()
        s = {n: sem(n) for n in names}
        (ident_in_s, const_in, wq_in, wk_in, wv_in, wo_in, x_in_s, y_in, y_out,
         absmax_done, absmax_all, winv_done, whi_done, wlo_done,
         sum_part, sum_done, sum_all, theta_done, neg_done, up_t, gate_t, down_t, coef_done, setup,
         mv_done, eps_done, pow_done, newton, rstd_done, xs_ready, xh_ready, xl_ready, xT_ready,
         xnT_ready,
         kv_ready, k_step, vh_done, kv_used, kr_ready, khi_done, klo_done, kT_ready, kstack_done,
         q_ready, q_step, qr_ready, qhi_done, qlo_done, qT_ready, qstack_done,
         mx_ready, mx_done, mh_done, ml_done, mT_ready, m_row_s, m_rows,
         sc_ready, exp_done, pl_ready, pv_done,
         up_ready, gate_ready, tanh_done, t1_done, h32_ready, hid_done,
         rden_done, e_done, ef_done, attn_done,
         aT_ready, attnT_ready, down_ready, wo_ready, y1_done, y_ready) = (s[n] for n in names)

        up_in, gate_in, down_in = ([sem(f"{w}_in{c}") for c in range(C)] for w in ("up", "gate", "down"))
        winv_step, coef_step, more_sum, own_neg, sign_step = (
            sem(n) for n in ("winv_step", "coef_step", "more_sum", "own_neg", "sign_step"))

        raws = (hid_raw, late, hid_raw)
        flat = (t_up[:, :, :].rearrange("p c e -> p (c e)"), t_gate[:, :, :].rearrange("p c e -> p (c e)"),
                as16(late[:, 0:4096]))
        PIECE = 3 * E // (H // 2 - 2)

        def down_piece(i):
            at = E + (i - 1) * PIECE
            return hid_raw[:, bass.ds(at, PIECE)], flat[2][:, bass.ds(at, PIECE)]

        BELOW_BY_DVE = ((0, 0), (0, 1))
        BELOW_BY_POOL = ((0, 2), (0, 3), (1, 0), (1, 1), (2, 0), (2, 1), (2, 2), (2, 3))
        SIGNS = ((1, 3), (1, 2))
        arrived, turned = (up_in, gate_in, down_in), (up_t, gate_t, down_t)

        block = ctx.enter_context(nc.Block())

        PAIRS = 3

        def all_pairs(eng, b, slot):
            def pair(i):
                for j in range(2):
                    h = 2 * i + j
                    slot(b, h, b * H + h, j, i)

            pair(0)
            with eng.Fori(0, (H // 2 - 2) // PAIRS) as i:
                for k in range(PAIRS):
                    pair(i * PAIRS + (k + 1))
            pair(H // 2 - 1)

        def is_(h, value):
            return isinstance(h, int) and h == value

        def ge(eng, s, value):
            if not isinstance(value, int) or value > 0:
                eng.wait_ge(s, value)

        @block.sync
        def _(sp):
            sp.dma_start(ident[:], ident_in).then_inc(ident_in_s, 16)
            sp.dma_start(x_in[:], x_v[0]).then_inc(x_in_s, 16)
            for w, s_in, lo, n in ((wk, wk_in, 512, 256), (wv, wv_in, 768, 256), (wq, wq_in, 0, 512)):
                sp.dma_start(w_raw[:, :, lo:lo + n], w.rearrange("(c p) n -> p c n", p=P)).then_inc(s_in, 16)
            sp.dma_start(cos_t[:], rope_c.rearrange("(t p) d -> p t d", p=P)).then_inc(const_in, 16)
            sp.dma_start(sin_t[:], rope_s.rearrange("(t p) d -> p t d", p=P)).then_inc(const_in, 16)
            for c in range(C):
                sp.dma_start(hid_raw[:, c * E:(c + 1) * E], w_up_t[c * P:(c + 1) * P, :]).then_inc(up_in[c], 16)
            for c in range(C):
                sp.dma_start(late[:, c * E:(c + 1) * E], w_gate_t[c * P:(c + 1) * P, :]).then_inc(gate_in[c], 16)
            sp.dma_start(wo_raw, wo.rearrange("(c p) n -> p c n", p=P)).then_inc(wo_in, 16)
            sp.wait_ge(xs_ready, T)
            sp.dma_start(x_in[:], x_v[1]).then_inc(x_in_s, 16)
            sp.wait_ge(up_t, C)
            down_v = w_down_t.rearrange("(e p) d -> p e d", p=P)
            hid_v = hid_raw[:, :].rearrange("p (e d) -> p e d", e=ET)
            for c in range(C):
                sp.dma_start(hid_v[:, c * 4:c * 4 + 4, :], down_v[:, c * 4:c * 4 + 4, :]).then_inc(down_in[c], 16)

            def rows_of_maxima(b):
                sp.wait_ge(m_row_s, b + 1)
                for part_ in range(2):
                    sp.dma_start(stk[STK + part_:STK + part_ + 1, 0:H, :],
                                 m_row[part_ * H:(part_ + 1) * H, :]).then_inc(m_rows, 16)

            rows_of_maxima(0)
            with sp.Fori(1, B) as b:
                ge(sp, y_out, (b - 1) * T * 16)
                sp.wait_ge(gate_t, C)
                sp.dma_start(y, x_v[b - 1]).then_inc(y_in, 16)
                sp.wait_ge(xs_ready, (b + 1) * T)
                sp.dma_start(x_in[:], x_v[(b + 1) % B]).then_inc(x_in_s, 16)
                rows_of_maxima(b)
                for t in range(T):
                    sp.wait_ge(y_ready, (b - 1) * T + t + 1)
                    sp.dma_start(out_v[b - 1, :, t, :], y[:, t, :]).then_inc(y_out, 16)
            sp.wait_ge(y_out, (B - 1) * T * 16)
            sp.dma_start(y, x_v[B - 1]).then_inc(y_in, 16)
            for t in range(T):
                sp.wait_ge(y_ready, (B - 1) * T + t + 1)
                sp.dma_start(out_v[B - 1, :, t, :], y[:, t, :]).then_inc(y_out, 16)
            sp.wait_ge(y_out, B * T * 16)

        def layernorm_rstd(pool, b=0):
            pool.wait_ge(eps_done, b + 1)
            nc.gpsimd.tensor_tensor(rstd[:, 1, :], rstd[:, 0, :], minus_half[:], ALU.pow).then_inc(pow_done, 1)

        def layernorm_lo(pool, b, t):
            pool.wait_ge(xh_ready, b * T + t + 1)
            nc.gpsimd.tensor_tensor(x_tok[:, t % 2, 1, :], xs32[:, t % 2, :], x_tok[:, t % 2, 0, :],
                                    ALU.subtract).then_inc(xl_ready, 1)

        def k_lo(pool, b, t):
            pool.wait_ge(khi_done, b * T + t + 1)
            nc.gpsimd.tensor_tensor(tk[t % 2][:, H:HA, 0:HD], r32[:, H:HA, :], tk[t % 2][:, H:HA, HD:2 * HD],
                                    ALU.subtract).then_inc(klo_done, 1)

        def q_lo(pool, b, t):
            pool.wait_ge(qhi_done, b * T + t + 1)
            nc.gpsimd.tensor_tensor(tk[t % 2][:, 0:H, 2 * HD:3 * HD], r32[:, 0:H, :],
                                    tk[t % 2][:, 0:H, HD:2 * HD], ALU.subtract).then_inc(qlo_done, 1)

        def hidden_pool(pool, n, j, e):
            pool.wait_ge(h32_ready, n + 1)
            nc.gpsimd.tensor_tensor(hid[:, e, 0, :], h32[:, j, :], one[:].to_broadcast([P, D]),
                                    ALU.mult).then_inc(hid_done, 1)
            pool.wait_ge(hid_done, 2 * n + 1)
            nc.gpsimd.tensor_tensor(hid[:, e, 1, :], h32[:, j, :], hid[:, e, 0, :],
                                    ALU.subtract).then_inc(hid_done, 1)

        def attn_pool(pool, n, j, h):
            pool.wait_ge(ef_done, n + 1)
            ge(pool, attn_done, 2 * n)
            nc.gpsimd.tensor_tensor(norm_a[:], norm_e[:, j], norm_f[:, j], ALU.add)
            hi = a_tok[:, 0, :, bass.ts(h, HD)]
            lo = a_tok[:, 1, :, bass.ts(h, HD)]
            nc.gpsimd.tensor_tensor(hi, norm_e[:, j], norm_f[:, j], ALU.add).then_inc(attn_done, 1)
            pool.wait_ge(attn_done, 2 * n + 1)
            nc.gpsimd.tensor_tensor(lo, norm_a[:], hi, ALU.subtract).then_inc(attn_done, 1)

        def slot_pool(b, h, n, j, g):
            if is_(h, 0):
                ge(nc.gpsimd, aT_ready, b * T)
                hidden_pool(nc.gpsimd, n, 0, 0)
            if not is_(h, H - 1):
                hidden_pool(nc.gpsimd, n + 1, 1 - j, h + 1)
            if not is_(h, 0):
                attn_pool(nc.gpsimd, n - 1, 1 - j, h - 1)

        def last_head_pool(pool, b):
            attn_pool(pool, b * H + H - 1, 1, H - 1)

        @block.gpsimd
        def _(pool):
            nc.gpsimd.memset(one[:], 1.0).then_inc(setup, 1)
            nc.gpsimd.memset(minus_half[:], -0.5).then_inc(setup, 1)
            nc.gpsimd.memset(v_all[:, :, :, 2 * HD:2 * HD + 1], 1.0).then_inc(setup, 1)
            pool.wait_ge(setup, 3)
            layernorm_rstd(pool, 0)
            layernorm_lo(pool, 0, 0)
            layernorm_lo(pool, 0, 1)
            pool.wait_ge(absmax_done, 3)
            nc.gpsimd.partition_all_reduce(wmax_all[:, 0:3], wmax[:, 0:3], P, RMAX).then_inc(absmax_all, 1)
            layernorm_lo(pool, 0, 2)
            layernorm_lo(pool, 0, 3)
            pool.wait_ge(wlo_done, 3)
            pool.wait_ge(xl_ready, T)
            nc.gpsimd.memset(stk[STK:ROWS, H:HA, :], -float(2 ** MAX_DOWN)).then_inc(setup, 1)
            pool.wait_ge(setup, 4)

            def sum_over_all(n):
                pool.wait_ge(sum_done, n + 1)
                nc.gpsimd.partition_all_reduce(total[:, n:n + 1], part[:, n:n + 1], P, RADD).then_inc(sum_all, 1)

            def below(n, c):
                part_ = slice(c * E, (c + 1) * E)
                pool.wait_ge(theta_done, 2 * n + 2)
                nc.gpsimd.tensor_scalar(flat[n][:, part_], raws[n][:, part_], ntheta[:, n:n + 1], None,
                                        ALU.is_lt).then_inc(neg_done, 1)

            def difference(k):
                n, c = SIGNS[k]
                part_ = slice(c * E, (c + 1) * E)
                pool.wait_ge(sign_step, 8 * (k + 1))
                nc.gpsimd.tensor_tensor(flat[n][:, part_], flat[n][:, part_], raws[n][:, part_],
                                        ALU.subtract).then_inc(turned[n], 1)

            sum_over_all(0)
            for t in range(T):
                k_lo(pool, 0, t)
            q_lo(pool, 0, 0)
            below(0, 2)
            below(0, 3)
            layernorm_rstd(pool, 1)
            q_lo(pool, 0, 1)
            sum_over_all(1)
            below(1, 0)
            below(1, 1)
            pool.wait_ge(absmax_done, 4)
            nc.gpsimd.partition_all_reduce(wmax_all[:, 3:4], wmax[:, 3:4], P, RMAX).then_inc(absmax_all, 1)
            q_lo(pool, 0, 2)
            difference(0)
            q_lo(pool, 0, 3)
            sum_over_all(2)
            pool.wait_ge(gate_t, 3)
            below(2, 0)
            below(2, 1)
            difference(1)
            below(2, 2)
            below(2, 3)
            all_pairs(pool, 0, slot_pool)
            last_head_pool(pool, 0)
            with pool.Fori(1, B) as b:
                for t in range(T):
                    layernorm_lo(pool, b, t)
                for t in range(T):
                    k_lo(pool, b, t)
                q_lo(pool, b, 0)
                layernorm_rstd(pool, b + 1)
                for t in range(1, T):
                    q_lo(pool, b, t)
                all_pairs(pool, b, slot_pool)
                last_head_pool(pool, b)

        def weight_parts():
            return [(w_raw[:, :, lo:lo + n], (w_qkv[:, 0, :, lo:lo + n], w_qkv[:, 1, :, lo:lo + n]))
                    for lo, n in ((0, 512), (512, 256), (768, 256))] + [
                        (wo_raw, (w_o[:, 0], w_o[:, 1]))]

        def front_act(act, b, also={}):
            def now(place):
                for f in also.get(place, ()):
                    f()

            first = isinstance(b, int)

            def hi_part(t):
                act.wait_ge(xs_ready, b * T + t + 1)
                if t >= 2:
                    act.wait_ge(xT_ready, b * T + t - 1)
                elif t == 0:
                    ge(act, pv_done, b * H)
                nc.scalar.copy(x_tok[:, t % 2, 0, :], xs32[:, t % 2, :]).then_inc(xh_ready, 1)

            def xn_out(t):
                act.wait_ge(xT_ready, b * T + t + 1)
                nc.scalar.copy(xn_t[:, :, :, t * P:(t + 1) * P].rearrange("p s c n -> p (s c) n"),
                               bank16(5 - t % 2).rearrange("p (k n) -> p k n", n=P)).then_inc(xnT_ready, 1)

            hi_part(0)
            hi_part(1)
            xn_out(0)
            if first:
                xn_out(1)
                hi_part(2)
                hi_part(3)
            else:
                hi_part(2)
                xn_out(1)
                hi_part(3)
            now("weights")
            xn_out(2)
            xn_out(3)
            now("k")
            for t in range(T):
                act.wait_ge(kr_ready, b * T + t + 1)
                ge(act, kT_ready, b * T + t - 1)
                stack = tk[t % 2]
                nc.scalar.copy(stack[:, H:HA, HD:2 * HD], r32[:, H:HA, :])
                nc.scalar.copy(stack[:, H:HA, 2 * HD:3 * HD], r32[:, H:HA, :]).then_inc(khi_done, 1)
                if t > 0:
                    k_out(act, b, t - 1)
            for t in range(T):
                act.wait_ge(qr_ready, b * T + t + 1)
                ge(act, qT_ready, (b * T + t - 1) * 2)
                stack = tk[t % 2]
                nc.scalar.copy(stack[:, 0:H, HD:2 * HD], r32[:, 0:H, :])
                nc.scalar.copy(stack[:, 0:H, 0:HD], r32[:, 0:H, :]).then_inc(qhi_done, 1)
                if t == 0:
                    k_out(act, b, T - 1)
                now(("q hi", t))
                for g in range(2):
                    n = (b * T + t) * 2 + g
                    act.wait_ge(qT_ready, n + 1)
                    nc.scalar.copy(stk[0:STK, 8 * g:8 * g + 8, t * P:(t + 1) * P],
                                   bank16(4)[0:STK, :].rearrange("p (h n) -> p h n", n=P)
                                   ).then_inc(qstack_done, 1)
                now(("q out", t))

        def k_out(act, b, t):
            act.wait_ge(kT_ready, b * T + t + 1)
            nc.scalar.copy(stk[0:STK, H:HA, t * P:(t + 1) * P],
                           bank16(4)[0:STK, :].rearrange("p (h n) -> p h n", n=P)).then_inc(kstack_done, 1)

        def maxima_act(act, b):
            act.wait_ge(mT_ready, b + 1)
            ge(act, m_rows, b * 32)
            nc.scalar.copy(m_row[:], bank16(0)[0:2 * H, 0:S]).then_inc(m_row_s, 1)

        def tanh_up(act, n, j):
            act.wait_ge(up_ready, n + 1)
            ge(act, t1_done, n - 1)
            nc.scalar.activation(th[:, j, :], psum[:, BU, :], ACT.Tanh, scale=TANH).then_inc(tanh_done, 1)

        def slot_act(b, h, n, j, g):
            act = nc.scalar
            if is_(h, 0):
                tanh_up(act, n + 1, 1)
            for half in range(2):
                act.wait_ge(sc_ready, 2 * n + half + 1)
                scores = psum[:, 2 * half:2 * half + 2, :]
                ge(act, pl_ready, 2 * n + half - 1)
                nc.scalar.activation(p32[:, half, :], scores, ACT.Exp, scale=SC)
                if half == 0:
                    ge(act, pv_done, n - 1)
                nc.scalar.activation(ph[:, j, 2 * half:2 * half + 2, :], scores, ACT.Exp,
                                     scale=SC).then_inc(exp_done, 1)
                if half == 0 and not is_(h, 0) and not is_(h, H - 1):
                    tanh_up(act, n + 1, 1 - j)

        @block.scalar
        def _(act):
            def hi_weights(n):
                src, dst = weight_parts()[n]
                nc.scalar.activation(dst[0], src, ACT.Copy, scale=winv[:, n:n + 1]).then_inc(whi_done, 1)

            def absolute_sums(n, c):
                nonlocal taken
                act.wait_ge(arrived[n][c], 16)
                for k in (2 * c, 2 * c + 1):
                    ge(act, sum_part, taken)
                    ge(act, sign_step, signs_taken)
                    taken += 1
                    nc.scalar.activation(psum[:, 6:8, :], raws[n][:, k * E // 2:(k + 1) * E // 2], ACT.Abs,
                                         accum_out=sums[:, n, k:k + 1]).then_inc(sum_part, 1)

            taken = signs_taken = 0

            def signs(k):
                nonlocal signs_taken
                n, c = SIGNS[k]
                act.wait_ge(theta_done, 2 * n + 2)
                act.wait_ge(sum_part, taken)
                for at in (c * E, c * E + E // 2):
                    part_ = slice(at, at + E // 2)
                    for side, dst in ((1.0, flat[n]), (-1.0, raws[n])):
                        ge(act, sign_step, signs_taken)
                        nc.scalar.activation(psum[:, 6:8, :], raws[n][:, part_], ACT.Relu,
                                             bias=ntheta[:, n:n + 1], scale=side).then_inc(sign_step, 1)
                        act.wait_ge(sign_step, signs_taken + 1)
                        nc.scalar.activation(dst[:, part_], psum[:, 6:8, :], ACT.Sign).then_inc(sign_step, 1)
                        signs_taken += 2

            def sums_of(n, *quarters):
                return [lambda c=c: absolute_sums(n, c) for c in quarters]

            front_act(act, 0, {
                "weights": [lambda: act.wait_ge(winv_done, 1)] + [lambda n=n: hi_weights(n) for n in (WK, WV, WQ)],
                "k": sums_of(0, 0, 1),
                ("q out", 0): sums_of(1, 0, 1, 2),
                ("q hi", 1): sums_of(1, 3),
                ("q out", 1): [lambda: signs(0)],
                ("q hi", 2): sums_of(2, 0, 1),
                ("q out", 2): sums_of(2, 2, 3),
                ("q out", 3): [lambda: signs(1)],
                ("q hi", 3): [lambda: act.wait_ge(winv_done, 2), lambda: hi_weights(WO)]})
            maxima_act(act, 0)
            act.wait_ge(coef_done, 1)
            tanh_up(act, 0, 0)
            all_pairs(act, 0, slot_act)
            with act.Fori(1, B) as b:
                front_act(act, b)
                maxima_act(act, b)
                tanh_up(act, b * H, 0)
                all_pairs(act, b, slot_act)

        def layernorm_stats(dve, b):
            dve.wait_ge(x_in_s, 16 * (b + 1))
            for t in range(T):
                nc.vector.bn_stats(stats[:, t, :], x_in[:, t, :]).then_inc(mv_done, 1)
            dve.wait_ge(mv_done, b * (2 * T) + T)
            nc.vector.memset(spare[:], 0.0)
            for t in range(T):
                nc.vector.bn_aggr(mv[:, t, :], stats[:, t, :]).then_inc(mv_done, 1)
            dve.wait_ge(mv_done, (b + 1) * (2 * T))
            nc.vector.tensor_scalar(rstd[:, 0, :], mv[:, :, 1], EPS, None, ALU.add).then_inc(eps_done, 1)

        def layernorm_scale(dve, b):
            dve.wait_ge(pow_done, b + 1)
            v, r, a, c, f = (rstd[:, k, :] for k in range(5))
            nc.vector.tensor_tensor(a, r, r, ALU.mult).then_inc(newton, 1)
            dve.wait_ge(newton, 3 * b + 1)
            nc.vector.tensor_tensor(c, a, v, ALU.mult).then_inc(newton, 1)
            dve.wait_ge(newton, 3 * b + 2)
            nc.vector.tensor_scalar(f, c, -0.5 * 2.0 ** X_UP, 1.5 * 2.0 ** X_UP, ALU.mult,
                                    ALU.add).then_inc(newton, 1)
            dve.wait_ge(newton, 3 * b + 3)
            nc.vector.tensor_tensor(rstd[:, 5, :], f, r, ALU.mult).then_inc(rstd_done, 1)

        def layernorm_apply(dve, b, t):
            if t == 0:
                dve.wait_ge(rstd_done, b + 1)
                ge(dve, pv_done, b * H - 1)
            if t >= 2:
                dve.wait_ge(xl_ready, b * T + t - 1)
            nc.vector.tensor_scalar(xs32[:, t % 2, :], x_in[:, t, :], mv[:, t, 0:1], rstd[:, 5, t:t + 1],
                                    ALU.subtract, ALU.mult).then_inc(xs_ready, 1)

        def rope(dve, b, t, src, h0, h1, between, step, ready, lo_done):
            n = b * T + t
            ge(dve, ready, n)
            for dst, tab in ((rope_a, cos_t), (rope_b, sin_t)):
                nc.vector.tensor_tensor(dst[:, h0:h1, :], src, tab[:, t:t + 1, :].to_broadcast([P, h1 - h0, HD]),
                                        ALU.mult).then_inc(step, 1)
            between()
            dve.wait_ge(step, 2 * (n + 1))
            ge(dve, lo_done, n)
            even, odd = slice(0, HD, 2), slice(1, HD, 2)
            nc.vector.tensor_tensor(r32[:, h0:h1, even], rope_a[:, h0:h1, even], rope_b[:, h0:h1, odd], ALU.add)
            nc.vector.tensor_tensor(r32[:, h0:h1, odd], rope_a[:, h0:h1, odd], rope_b[:, h0:h1, even],
                                    ALU.add).then_inc(ready, 1)

        def kv_dve(dve, b, t):
            n = b * T + t
            if isinstance(b, int) and t == 0:
                dve.wait_ge(const_in, 32)
            dve.wait_ge(kv_ready, n + 1)
            k = psum[:, t, 0:KV * HD].rearrange("p (h d) -> p h d", d=HD)
            v = psum[:, t, KV * HD:].rearrange("p (h d) -> p h d", d=HD)
            if t == 0 and not isinstance(b, int):
                dve.wait_ge(pl_ready, b * 2 * H)

            def v_parts():
                vl, vh = v_all[:, t, :, 0:HD], v_all[:, t, :, HD:2 * HD]
                down = 2.0 ** -(X_UP + W_UP)
                nc.vector.tensor_scalar(vh, v, down, None, ALU.mult).then_inc(vh_done, 1)
                dve.wait_ge(vh_done, n + 1)
                nc.vector.scalar_tensor_tensor(vl, v, down, vh, ALU.mult, ALU.subtract).then_inc(kv_used, 1)

            rope(dve, b, t, k, H, HA, v_parts, k_step, kr_ready, klo_done)

        def q_dve(dve, b, t):
            dve.wait_ge(q_ready, b * T + t + 1)
            rope(dve, b, t, psum[:, 5, :].rearrange("p (h d) -> p h d", d=HD), 0, H, lambda: None,
                 q_step, qr_ready, qlo_done)

        def attn_t_dve(dve, b, t):
            dve.wait_ge(aT_ready, (b - 1) * T + t + 1)
            if t == 0:
                dve.wait_ge(hid_done, b * 2 * H)
            nc.vector.tensor_copy(a_t[:, :, :, t * P:(t + 1) * P].rearrange("p s c n -> p (s c) n"),
                                  bank16(t).rearrange("p (k n) -> p k n", n=P)).then_inc(attnT_ready, 1)

        def maxima_dve(dve, b, between):
            for g in range(MAX_GROUPS):
                t, h = g // KV, g % KV * 2
                dve.wait_ge(mx_ready, b * MAX_GROUPS + g + 1)
                nc.vector.tensor_reduce(mx[:, t, h:h + 2], psum[:, 2 * (g % 2):2 * (g % 2) + 2, :], AX.X,
                                        ALU.max).then_inc(mx_done, 1)
                if g % KV == Q_ROPE and t + 1 < T:
                    q_dve(dve, b, t + 1)
                for f in between.get(g, ()):
                    f()
            down = 2.0 ** -MAX_DOWN
            dve.wait_ge(mx_done, (b + 1) * MAX_GROUPS)
            nc.vector.tensor_scalar(m_tok[:, :, 0, :], mx[:], down, None, ALU.mult).then_inc(mh_done, 1)
            dve.wait_ge(mh_done, b + 1)
            nc.vector.scalar_tensor_tensor(m_tok[:, :, 1, :], mx[:], down, m_tok[:, :, 0, :], ALU.mult,
                                           ALU.subtract).then_inc(ml_done, 1)
            for f in between.get(MAX_GROUPS, ()):
                f()

        def y_after(dve, b):
            ends = [2 * ET * (t + 1) for t in range(T - 1)]
            ends += [ends[-1] + 3 * C * (t + 1) for t in range(T)]
            steps = [lambda t=t: y_down(dve, b, t) for t in range(1, T)]
            steps += [lambda t=t: y_attn(dve, b, t) for t in range(T)]
            at = {1: [lambda: layernorm_scale(dve, b + 1)]}
            for end, step in zip(ends, steps):
                g = next((g for g in range(MAX_GROUPS) if sum(BEFORE) + sum(BESIDE[:g + 1]) >= end), MAX_GROUPS)
                at.setdefault(min(g + Y_LATE, MAX_GROUPS), []).append(step)
            return at

        def y_down(dve, b, t):
            n = (b - 1) * T + t
            dve.wait_ge(down_ready, n + 1)
            nc.vector.scalar_tensor_tensor(y[:, t, :], psum[:, DOWN_BANK[t], :], CD, y[:, t, :], ALU.mult,
                                           ALU.add).then_inc(y1_done, 1)

        def y_attn(dve, b, t):
            n = (b - 1) * T + t
            dve.wait_ge(wo_ready, n + 1)
            dve.wait_ge(y1_done, n + 1)
            nc.vector.scalar_tensor_tensor(y[:, t, :], psum[:, WO_BANK[t], :], CA, y[:, t, :], ALU.mult,
                                           ALU.add).then_inc(y_ready, 1)

        def normalise(dve, n, j):
            dve.wait_ge(pv_done, n + 1)
            o = psum[:, 6 + j, 0:T * (2 * HD + 1)].rearrange("p (t d) -> p t d", t=T)
            ge(dve, ef_done, n)
            nc.vector.reciprocal(rden[:], o[:, :, 2 * HD:2 * HD + 1]).then_inc(rden_done, 1)
            dve.wait_ge(rden_done, n + 1)
            ge(dve, attn_done, 2 * (n - 1))
            r = rden[:].to_broadcast([P, T, HD])
            nc.vector.tensor_tensor(norm_e[:, j], o[:, :, 0:HD], r, ALU.mult).then_inc(e_done, 1)
            dve.wait_ge(e_done, n + 1)
            nc.vector.tensor_tensor(norm_f[:, j], o[:, :, HD:2 * HD], r, ALU.mult).then_inc(ef_done, 1)

        def hidden_dve(dve, n, j):
            dve.wait_ge(tanh_done, n + 1)
            ge(dve, h32_ready, n)
            nc.vector.scalar_tensor_tensor(t1, th[:, j, :], 1.0, psum[:, BU, :], ALU.add,
                                           ALU.mult).then_inc(t1_done, 1)
            dve.wait_ge(t1_done, n + 1)
            dve.wait_ge(gate_ready, n + 1)
            ge(dve, hid_done, 2 * (n - 1))
            nc.vector.scalar_tensor_tensor(h32[:, j, :], t1, 2.0 ** -(H_DOWN + 2 * X_UP), psum[:, BG, :],
                                           ALU.mult, ALU.mult).then_inc(h32_ready, 1)

        def slot_dve(b, h, n, j, g):
            dve = nc.vector

            def lo_part(half):
                dve.wait_ge(exp_done, 2 * n + half + 1)
                if half == 0:
                    ge(dve, pv_done, n - 1)
                nc.vector.tensor_tensor(pl[:, j, 2 * half:2 * half + 2, :].rearrange("p a b -> p (a b)"),
                                        p32[:, half, :],
                                        ph[:, j, 2 * half:2 * half + 2, :].rearrange("p a b -> p (a b)"),
                                        ALU.subtract).then_inc(pl_ready, 1)

            if not is_(h, 0):
                lo_part(0)
            if not is_(h, H - 1):
                hidden_dve(dve, n + 1, 1 - j)
            if is_(h, 0):
                lo_part(0)
            lo_part(1)
            if not is_(h, 0):
                normalise(dve, n - 1, 1 - j)
            if isinstance(b, int) and is_(h, 1):
                dve.wait_ge(neg_done, len(BELOW_BY_POOL))
            if isinstance(b, int) and j == 0 and not isinstance(h, int):
                raw, tern = down_piece(g)
                nc.vector.scalar_tensor_tensor(tern, raw, theta[:, 2:3], tern, ALU.is_gt,
                                               ALU.subtract).then_inc(down_t, 1)

        def last_head_dve(dve, b):
            normalise(dve, b * H + H - 1, 1)

        @block.vector
        def _(dve):
            def largest(n, s_in):
                dve.wait_ge(s_in, 16)
                nc.vector.tensor_reduce(wmax[:, n:n + 1], weight_parts()[n][0], AX.XY, ALU.max,
                                        apply_absolute_value=True).then_inc(absmax_done, 1)

            def exponents(lo, hi, k):
                some = slice(lo, hi)
                dve.wait_ge(absmax_all, k + 1)
                nc.vector.tensor_scalar(wmax_all[:, some], wmax_all[:, some], 2.0 ** -100, 2.0 ** 100,
                                        ALU.max, ALU.min).then_inc(winv_step, 1)
                dve.wait_ge(winv_step, 3 * k + 1)
                nc.vector.tensor_scalar(wpow[:, some].bitcast(U32), wmax_all[:, some].bitcast(U32),
                                        0x7F800000, None, ALU.bitwise_and).then_inc(winv_step, 1)
                dve.wait_ge(winv_step, 3 * k + 2)
                nc.vector.reciprocal(winv[:, some], wpow[:, some]).then_inc(winv_step, 1)
                dve.wait_ge(winv_step, 3 * k + 3)
                nc.vector.tensor_scalar(winv[:, some], winv[:, some], 2.0 ** W_UP, None,
                                        ALU.mult).then_inc(winv_done, 1)
                dve.wait_ge(winv_done, k + 1)

            def lo_weights(n):
                src, dst = weight_parts()[n]
                dve.wait_ge(whi_done, (3, 1, 2, 4)[n])
                nc.vector.scalar_tensor_tensor(dst[1], src, winv[:, n:n + 1], dst[0], ALU.mult,
                                               ALU.subtract).then_inc(wlo_done, 1)

            def more_sums(n, c):
                dve.wait_ge(arrived[n][c], 16)
                nc.vector.tensor_reduce(sums[:, n, 2 * c:2 * c + 2],
                                        raws[n][:, c * E:(c + 1) * E].rearrange("p (g k) -> p g k", g=2), AX.X, ALU.add,
                                        apply_absolute_value=True).then_inc(more_sum, 1)

            def thresholds(n, by_act, by_dve):
                dve.wait_ge(sum_part, by_act)
                ge(dve, more_sum, by_dve)
                nc.vector.tensor_reduce(part[:, n:n + 1], sums[:, n, :], AX.X, ALU.add).then_inc(sum_done, 1)
                dve.wait_ge(sum_all, n + 1)
                nc.vector.tensor_scalar(scale[:, n:n + 1], total[:, n:n + 1], 1.0 / (E * D), 1e-8, ALU.mult,
                                        ALU.add).then_inc(theta_done, 1)
                dve.wait_ge(theta_done, 2 * n + 1)
                nc.vector.tensor_scalar(theta[:, n:n + 1], scale[:, n:n + 1], 0.5, None, ALU.mult)
                nc.vector.tensor_scalar(ntheta[:, n:n + 1], scale[:, n:n + 1], -0.5, None,
                                        ALU.mult).then_inc(theta_done, 1)
                dve.wait_ge(theta_done, 2 * n + 2)

            def ternary(n, c):
                nonlocal own
                part_ = slice(c * E, (c + 1) * E)
                if (n, c) in BELOW_BY_DVE:
                    nc.vector.tensor_scalar(flat[n][:, part_], raws[n][:, part_], ntheta[:, n:n + 1], None,
                                            ALU.is_lt).then_inc(own_neg, 1)
                    own += 1
                    dve.wait_ge(own_neg, own)
                else:
                    dve.wait_ge(neg_done, BELOW_BY_POOL.index((n, c)) + 1)
                nc.vector.scalar_tensor_tensor(flat[n][:, part_], raws[n][:, part_], theta[:, n:n + 1],
                                               flat[n][:, part_], ALU.is_gt,
                                               ALU.subtract).then_inc(turned[n], 1)

            def coefficients():
                def step(out_, a, b_):
                    nonlocal k
                    nc.vector.tensor_tensor(out_, a, b_, ALU.mult).then_inc(coef_step, 1)
                    k += 1
                    dve.wait_ge(coef_step, k)
                k = 0
                step(coef[:, 4:5], wpow[:, WQ:WQ + 1], wpow[:, WK:WK + 1])
                step(coef[:, 5:6], wpow[:, WV:WV + 1], wpow[:, WO:WO + 1])
                step(coef[:, 6:7], scale[:, 0:1], scale[:, 1:2])
                step(coef[:, 7:8], coef[:, 6:7], scale[:, 2:3])
                nc.vector.tensor_scalar(SC, coef[:, 4:5], float(HD) ** -0.5, None, ALU.mult)
                nc.vector.tensor_scalar(TANH, scale[:, 0:1], 0.5 * 2.0 ** -X_UP, None, ALU.mult)
                nc.vector.tensor_scalar(CD, coef[:, 7:8], 2.0 ** (H_DOWN - 1), None, ALU.mult)
                nc.vector.tensor_scalar(CA, coef[:, 5:6], 2.0 ** -W_UP, None, ALU.mult).then_inc(coef_done, 1)

            own = 0
            layernorm_stats(dve, 0)
            largest(WK, wk_in)
            layernorm_scale(dve, 0)
            layernorm_apply(dve, 0, 0)
            layernorm_apply(dve, 0, 1)
            largest(WV, wv_in)
            largest(WQ, wq_in)
            layernorm_apply(dve, 0, 2)
            layernorm_apply(dve, 0, 3)
            exponents(0, 3, 0)
            for n in (WK, WV, WQ):
                lo_weights(n)
            more_sums(0, 2)
            more_sums(0, 3)
            kv_dve(dve, 0, 0)
            thresholds(0, 4, 2)
            for t in range(1, T):
                kv_dve(dve, 0, t)
            q_dve(dve, 0, 0)
            ternary(0, 0)
            ternary(0, 1)
            layernorm_stats(dve, 1)
            maxima_dve(dve, 0, {
                1: [lambda: ternary(0, 2)],
                2: [lambda: layernorm_scale(dve, 1)],
                4: [lambda: ternary(0, 3)],
                3: [lambda: thresholds(1, 4 + 2 * C, 2)],
                7: [lambda: largest(3, wo_in)],
                11: [lambda: ternary(1, 0)],
                13: [lambda: ternary(1, 1)],
                15: [lambda: exponents(3, 4, 1)],
                20: [lambda: thresholds(2, 4 + 4 * C, 2), coefficients],
                23: [lambda: lo_weights(3)],
                MAX_GROUPS: [lambda: ternary(2, 0)]})
            hidden_dve(dve, 0, 0)
            all_pairs(dve, 0, slot_dve)
            with dve.Fori(1, B) as b:
                layernorm_apply(dve, b, 0)
                layernorm_apply(dve, b, 1)
                last_head_dve(dve, b - 1)
                dve.wait_ge(y_in, 16 * b)
                y_down(dve, b, 0)
                layernorm_apply(dve, b, 2)
                layernorm_apply(dve, b, 3)
                for t in range(T):
                    kv_dve(dve, b, t)
                q_dve(dve, b, 0)
                for t in range(T):
                    attn_t_dve(dve, b, t)
                layernorm_stats(dve, b + 1)
                maxima_dve(dve, b, y_after(dve, b))
                hidden_dve(dve, b * H, 0)
                all_pairs(dve, b, slot_dve)
            last_head_dve(dve, B - 1)
            dve.wait_ge(y_in, 16 * B)
            y_down(dve, B, 0)
            for t in range(T):
                attn_t_dve(dve, B, t)
            for t in range(1, T):
                y_down(dve, B, t)
            for t in range(T):
                y_attn(dve, B, t)

        def pe_front(pe, b):
            first = isinstance(b, int)

            def transpose8(bank, src, inc):
                for k in range(8):
                    m = nc.tensor.transpose(bank16(bank)[:, k * P:(k + 1) * P], src(k), ident[:])
                m.then_inc(inc, 1)

            def x_t(t):
                pe.wait_ge(xl_ready, b * T + t + 1)
                if t >= 2:
                    pe.wait_ge(xnT_ready, b * T + t - 1)
                elif t == 0:
                    ge(pe, h32_ready, b * H)
                elif not first:
                    pe.wait_ge(y1_done, (b - 1) * T + 1)
                transpose8(5 - t % 2, lambda k: x_tok[:, t % 2, k // C, (k % C) * P:(k % C + 1) * P],
                           xT_ready)

            def kv(t):
                pe.wait_ge(xnT_ready, b * T + t + 1)
                if t == 0:
                    ge(pe, exp_done, b * 2 * H)
                projection(t, t, slice(512, 1024), kv_ready, range(3 * C))

            def projection(t, bank, cols, done, steps):
                for k in steps:
                    c, (xp, wp) = k // 3, ((0, 0), (0, 1), (1, 0))[k % 3]
                    m = nc.tensor.matmul(psum[:, bank, :], xn_t[:, xp, c, t * P:(t + 1) * P],
                                         w_qkv[:, wp, c, cols], start=k == 0, stop=k == 3 * C - 1)
                    if k == 3 * C - 1:
                        m.then_inc(done, 1)

            def q(t, steps=range(3 * C)):
                if 0 in steps and t == 0 and first:
                    pe.wait_ge(wlo_done, 3)
                if 0 in steps and t == 0:
                    pe.wait_ge(xnT_ready, (b + 1) * T)
                elif 0 in steps:
                    pe.wait_ge(q_step, 2 * (b * T + t))
                projection(t, 5, slice(0, 512), q_ready, steps)

            def stack_t(src, done):
                for h in range(8):
                    m = nc.tensor.transpose(bank16(4)[0:STK, h * P:(h + 1) * P], src[:, h, :], ident[:])
                m.then_inc(done, 1)

            def k_t(t):
                pe.wait_ge(klo_done, b * T + t + 1)
                if t == 0:
                    pe.wait_ge(xnT_ready, (b + 1) * T)
                else:
                    pe.wait_ge(kstack_done, b * T + t)
                stack_t(tk[t % 2][:, H:HA, :], kT_ready)

            def q_t(t, g):
                pe.wait_ge(qlo_done, b * T + t + 1)
                if t == 0 and g == 0:
                    pe.wait_ge(kstack_done, (b + 1) * T)
                else:
                    pe.wait_ge(qstack_done, (b * T + t) * 2 + g)
                stack_t(tk[t % 2][:, 8 * g:8 * g + 8, :], qT_ready)

            def maxima(g):
                t, i = g // KV, g % KV
                if i == 0:
                    pe.wait_ge(qstack_done, (b * T + t + 1) * 2)
                if g == 0:
                    pe.wait_ge(kstack_done, (b + 1) * T)
                    pe.wait_ge(kv_used, (b + 1) * T)
                    ge(pe, attnT_ready, b * T)
                if g >= 2:
                    pe.wait_ge(mx_done, b * MAX_GROUPS + g - 1)
                for u in range(2):
                    m = nc.tensor.matmul(psum[:, 2 * (g % 2) + u, :],
                                         stk[0:STK, 2 * i + u, t * P:(t + 1) * P],
                                         stk[0:STK, H + i, :], start=True, stop=True)
                m.then_inc(mx_ready, 1)

            if first:
                tail = []
            else:
                tail = [f for t in (1, 2, 3) for f in down_steps(pe, b, t)]
                tail += [f for t in range(T) for f in wo_steps(pe, b, t)]

            def some(n):
                run_tail(pe, tail[:n])
                del tail[:n]

            if first:
                pe.wait_ge(ident_in_s, 16)
                for t in range(T):
                    x_t(t)
                pe.wait_ge(wlo_done, 2)
            else:
                run_tail(pe, down_steps(pe, b, 0)[PE_EARLY:])
                some(BEFORE[0])
                x_t(0)
                x_t(1)
                kv(0)
                x_t(2)
                kv(1)
                x_t(3)
            if first:
                kv(0)
                kv(1)
            kv(2)
            k_t(0)
            kv(3)
            k_t(1)
            q(0)
            k_t(2)
            if not first:
                for t in range(T):
                    attn_t_pe(pe, b, t)
            k_t(3)
            some(BEFORE[1])
            q_t(0, 0)
            some(BEFORE[2])
            q_t(0, 1)
            q(1)
            for g in range(MAX_GROUPS):
                maxima(g)
                t, i = g // KV, g % KV
                if i >= KV // 2 and t + 2 < T:
                    q(t + 2, range((i - KV // 2) * 3, (i - KV // 2) * 3 + 3))
                some(BESIDE[g])
                if i in (Q_TRANSPOSE, Q_TRANSPOSE + 1) and t + 1 < T:
                    q_t(t + 1, i - Q_TRANSPOSE)
            some(len(tail))
            if first:
                pe.wait_ge(up_t, C)
            up_pe(pe, b * H, 0)
            pe.wait_ge(ml_done, b + 1)
            for t in range(T):
                m = nc.tensor.transpose(bank16(0)[0:2 * H, t * P:(t + 1) * P],
                                        m_tok[:, t, :, :].rearrange("p s h -> p (s h)"), ident[:])
            m.then_inc(mT_ready, 1)

        def run_tail(pe, steps):
            for step in steps:
                step()

        def attn_t_pe(pe, b, t):
            if t == 0:
                pe.wait_ge(attn_done, b * 2 * H)
                pe.wait_ge(exp_done, b * 2 * H)
            if not isinstance(b, int):
                pe.wait_ge(kv_used, b * T + t + 1)
            for k in range(8):
                m = nc.tensor.transpose(bank16(t)[:, k * P:(k + 1) * P],
                                        a_tok[:, k // C, t, (k % C) * P:(k % C + 1) * P], ident[:])
            m.then_inc(aT_ready, 1)

        def down_steps(pe, b, t):
            def step(k):
                def go():
                    e, s_ = k // 2, k % 2
                    if t == 0 and k == 0:
                        pe.wait_ge(t1_done, b * H)
                        pe.wait_ge(hid_done, b * 2 * H)
                    if t in (1, 2) and k == 0:
                        pe.wait_ge(ef_done, b * H)
                    if t == 3 and k == 0:
                        pe.wait_ge(y1_done, (b - 1) * T + 2)
                    m = nc.tensor.matmul(psum[:, DOWN_BANK[t], :], hid[:, e, s_, t * P:(t + 1) * P],
                                         t_down[:, e, :], start=k == 0, stop=k == 2 * ET - 1)
                    if k == 2 * ET - 1:
                        m.then_inc(down_ready, 1)
                return go
            return [step(k) for k in range(2 * ET)]

        def wo_steps(pe, b, t):
            def step(k):
                def go():
                    c, (ap, wp) = k // 3, ((0, 0), (0, 1), (1, 0))[k % 3]
                    if k == 0 and t == 0:
                        pe.wait_ge(attnT_ready, b * T)
                    if k == 0 and t < 2:
                        pe.wait_ge(y1_done, (b - 1) * T + t + 3)
                    if k == 0 and t >= 2:
                        pe.wait_ge(y_ready, (b - 1) * T + t - 1)
                    m = nc.tensor.matmul(psum[:, WO_BANK[t], :], a_t[:, ap, c, t * P:(t + 1) * P],
                                         w_o[:, wp, c, :], start=k == 0, stop=k == 3 * C - 1)
                    if k == 3 * C - 1:
                        m.then_inc(wo_ready, 1)
                return go
            return [step(k) for k in range(3 * C)]

        def pe_pv(pe, n, j, g):
            pe.wait_ge(pl_ready, 2 * n + 2)
            ge(pe, ef_done, n - 1)
            for t in range(T):
                at, mid, end = (t * (2 * HD + 1) + k for k in (0, HD, 2 * HD + 1))
                q_ = slice(t * P, (t + 1) * P)
                for kt in range(T):
                    nc.tensor.matmul(psum[:, 6 + j, at:end], ph[:, j, kt, q_], v_all[:, kt, g, :],
                                     start=kt == 0, stop=False)
                for kt in range(T):
                    m = nc.tensor.matmul(psum[:, 6 + j, mid:end], pl[:, j, kt, q_], v_all[:, kt, g, HD:],
                                         start=False, stop=kt == T - 1)
            m.then_inc(pv_done, 1)

        def pe_last(pe, b):
            run_tail(pe, down_steps(pe, b, 0)[:PE_EARLY])
            pe_pv(pe, b * H - 1, 1, KV - 1)

        def scores_pe(pe, b, n, h, g, half):
            if not is_(h, 0):
                pe.wait_ge(exp_done, 2 * (n - 1) + half + 1)
            elif half == 0:
                pe.wait_ge(m_row_s, b + 1)
                pe.wait_ge(m_rows, 32 * (b + 1))
            for kt in (2 * half, 2 * half + 1):
                m = nc.tensor.matmul(psum[:, kt, :], stk[0:ROWS, H + g, kt * P:(kt + 1) * P],
                                     stk[0:ROWS, h, :], start=True, stop=True)
            m.then_inc(sc_ready, 1)

        def up_pe(pe, n, h):
            ge(pe, t1_done, n)
            ternary_product(t_up, BU, h, up_ready)

        def gate_pe(pe, n, h):
            ge(pe, h32_ready, n)
            ternary_product(t_gate, BG, h, gate_ready)

        def ternary_product(w, bank, h, done):
            for c in range(C):
                for s_ in range(2):
                    m = nc.tensor.matmul(psum[:, bank, :], w[:, c, bass.ts(h, P)], xn_t[:, s_, c, :],
                                         start=c == 0 and s_ == 0, stop=c == C - 1 and s_ == 1)
            m.then_inc(done, 1)

        def slot_pe(b, h, n, j, g):
            pe = nc.tensor
            if is_(h, 0):
                if isinstance(b, int):
                    pe.wait_ge(gate_t, C)
                    pe.wait_ge(setup, 4)
                gate_pe(pe, n, 0)
                up_pe(pe, n + 1, 1)
                scores_pe(pe, b, n, h, g, 0)
                scores_pe(pe, b, n, h, g, 1)
                gate_pe(pe, n + 1, 1)
                return
            if is_(h, 1):
                up_pe(pe, n + 1, h + 1)
            scores_pe(pe, b, n, h, g, 0)
            if is_(h, 1):
                scores_pe(pe, b, n, h, g, 1)
                gate_pe(pe, n + 1, h + 1)
                ge(pe, y_ready, b * T)
            else:
                scores_pe(pe, b, n, h, g, 1)
                if not is_(h, H - 1):
                    up_pe(pe, n + 1, h + 1)
                    gate_pe(pe, n + 1, h + 1)
            pe_pv(pe, n - 1, 1 - j, g if j else g - 1)

        @block.tensor
        def _(pe):
            pe_front(pe, 0)
            all_pairs(pe, 0, slot_pe)
            pe.wait_ge(down_t, 1 + H // 2 - 2)
            pe_last(pe, 1)
            with pe.Fori(1, B) as b:
                pe_front(pe, b)
                all_pairs(pe, b, slot_pe)
                pe_last(pe, b + 1)
            run_tail(pe, down_steps(pe, B, 0)[PE_EARLY:])
            run_tail(pe, down_steps(pe, B, 1))
            for t in range(T):
                attn_t_pe(pe, B, t)
            for t in (2, 3):
                run_tail(pe, down_steps(pe, B, t))
            for t in range(T):
                run_tail(pe, wo_steps(pe, B, t))


def rope_tables():
    inv_freq = (1.0 / np.float32(10000.0) ** (np.arange(0, HD, 2, dtype=np.float32) / np.float32(HD))).astype(np.float32)
    angle = (np.arange(S, dtype=np.float32)[:, None] * inv_freq[None, :]).astype(np.float32)
    down = np.float32(2.0 ** -(X_UP + W_UP))
    cos, sin = np.cos(angle) * down, np.sin(angle) * down
    c = np.repeat(cos, 2, axis=1).astype(np.float32)
    sn = np.stack([sin, -sin], axis=2).reshape(S, HD).astype(np.float32)
    return c, sn


def kernel(L0_attn_x, L0_attn_wq, L0_attn_wk, L0_attn_wv, L0_attn_wo, L0_ffn_W_up, L0_ffn_W_gate, L0_ffn_W_down):
    import concourse.bacc as bacc
    from concourse.bass_utils import run_bass_kernel_spmd

    c, sn = rope_tables()
    arrays = {
        "x": L0_attn_x, "wq": L0_attn_wq, "wk": L0_attn_wk, "wv": L0_attn_wv, "wo": L0_attn_wo,
        "w_up_t": np.asarray(L0_ffn_W_up).T, "w_gate_t": np.asarray(L0_ffn_W_gate).T,
        "w_down_t": np.asarray(L0_ffn_W_down).T,
        "rope_c": c, "rope_s": sn, "ident": np.eye(P, dtype=np.float16),
    }
    arrays = {k: np.ascontiguousarray(v) for k, v in arrays.items()}
    nc = bacc.Bacc("TRN2", target_bir_lowering=False, num_devices=1)
    aps = [nc.dram_tensor(k, v.shape, mybir.dt.from_np(v.dtype), kind="ExternalInput").ap()
           for k, v in arrays.items()]
    out = nc.dram_tensor("out", (B, S, D), F32, kind="ExternalOutput").ap()
    build(nc, *aps, out)
    r = run_bass_kernel_spmd(nc, [arrays], core_ids=[0])
    return r.results[0]["out"]
```
